# Optimizing a Trainium2 kernel written in Bass

```python
import numpy as np
import jax
import jax.numpy as jnp

def _softmax(x, axis=-1):
    return jax.nn.softmax(x, axis=axis)

def _gelu(x):
    return jax.nn.gelu(x, approximate=True)

def _silu(x):
    return jax.nn.silu(x)

def _sigmoid(x):
    return jax.nn.sigmoid(x)

def _layernorm(x, axis=-1, eps=1e-05):
    m = jnp.mean(x, axis=axis, keepdims=True)
    v = jnp.var(x, axis=axis, keepdims=True)
    return (x - m) / jnp.sqrt(v + eps)

def _scatter_add(tgt, idx, src, axis=0):
    return tgt.at[idx].add(src)

def _segment_sum(src, seg, n):
    return jax.ops.segment_sum(src, seg, n)
kernel_name = 'mk_flamingo_gated_d1_seqx_r8_ab9dc0'

def setup_inputs(seed: int=0):
    np.random.seed(seed)
    _w = jnp.asarray

    def _rec_inputs():
        import jax
        import jax.numpy as jnp
        _rk = jax.random.key(seed)
        x = 7.22e-05 + 1 * jax.random.normal(jax.random.fold_in(_rk, 1), (64, 64, 128), jnp.float32)
        _lenS = 64 - jax.random.randint(jax.random.fold_in(_rk, 7), (64,), 0, max(1, 64 // 4) + 1, jnp.int32)
        _lenS2 = 64 - jax.random.randint(jax.random.fold_in(_rk, 8), (64,), 0, max(1, 64 // 4) + 1, jnp.int32)
        _ctx_1024P = jax.random.normal(jax.random.fold_in(_rk, 11), (64, 16, 128), jnp.float32)
        _ctx_1024c = jax.random.dirichlet(jax.random.fold_in(_rk, 511), 0.3 * jnp.ones((16,), jnp.float32), (64, 64))
        _ctx_1024t = jnp.einsum('bsk,bkd->bsd', _ctx_1024c, _ctx_1024P)
        _ctx_1024t = _ctx_1024t * jax.lax.rsqrt(jnp.mean(jnp.square(_ctx_1024t)) + 1e-12) * 0.953939
        ctx_1024 = 4.13588e-05 + 0.999923 * (_ctx_1024t + 0.3 * jax.random.normal(jax.random.fold_in(_rk, 611), (64, 64, 128), jnp.float32))
        _g = jax.random.normal(jax.random.fold_in(_rk, 9001), (2, 1), jnp.float32)
        _g = jnp.sign(_g) * jnp.maximum(jnp.abs(_g), 1.0) + (_g == 0) * 1.0
        g_xattn = _g[0]
        g_ffn = _g[1]
        return (x, ctx_1024, g_xattn, g_ffn)
    x, ctx_1024, g_xattn, g_ffn = _rec_inputs()

    def _L0_xattn_setup():
        import jax, jax.numpy as jnp
        import numpy as np
        N_HEADS = 16
        key = jax.random.key(seed)
        ks = jax.random.split(key, 12)
        B, L, D = (4, 256, 128)
        s = 1.0 / np.sqrt(D)
        return {'queries': jax.random.normal(ks[0], (B, L, D), dtype=jnp.float32), 'keys': jax.random.normal(ks[1], (B, L, D), dtype=jnp.float32), 'values': jax.random.normal(ks[2], (B, L, D), dtype=jnp.float32), 'Wq': jax.random.normal(ks[3], (D, D), dtype=jnp.float32) * s, 'bq': jnp.zeros((D,), dtype=jnp.float32), 'Wk': jax.random.normal(ks[4], (D, D), dtype=jnp.float32) * s, 'bk': jnp.zeros((D,), dtype=jnp.float32), 'Wv': jax.random.normal(ks[5], (D, D), dtype=jnp.float32) * s, 'bv': jnp.zeros((D,), dtype=jnp.float32), 'Wo': jax.random.normal(ks[6], (D, D), dtype=jnp.float32) * s, 'bo': jnp.zeros((D,), dtype=jnp.float32)}
    _L0_xattn_all = _L0_xattn_setup()
    _L0_xattn_in = {k: v for k, v in _L0_xattn_all.items() if k in ('Wq', 'bq', 'Wk', 'bk', 'Wv', 'bv', 'Wo', 'bo')}
    del _L0_xattn_all

    def _L0_ffn_setup():
        import jax, jax.numpy as jnp
        import numpy as np
        H, I, E_ROUTED, TOP_K = (128, 352, 7, 2)
        B, S = (4, 256)

        def _expert(h, g, u, d):
            return jnp.einsum('...i,hi->...h', jax.nn.silu(h @ g.T) * (h @ u.T), d)
        key = jax.random.key(seed)
        ks = jax.random.split(key, 10)
        sc = 0.02
        return {'x': jax.random.normal(ks[0], (B, S, H), dtype=jnp.float32), 'sg': jax.random.normal(ks[1], (I, H), dtype=jnp.float32) * sc, 'su': jax.random.normal(ks[2], (I, H), dtype=jnp.float32) * sc, 'sd': jax.random.normal(ks[3], (H, I), dtype=jnp.float32) * sc, 'rg': jax.random.normal(ks[4], (E_ROUTED, I, H), dtype=jnp.float32) * sc, 'ru': jax.random.normal(ks[5], (E_ROUTED, I, H), dtype=jnp.float32) * sc, 'rd': jax.random.normal(ks[6], (E_ROUTED, H, I), dtype=jnp.float32) * sc, 'wr': jax.random.normal(ks[7], (E_ROUTED, H), dtype=jnp.float32) * sc, 'rb': jnp.zeros((E_ROUTED,), dtype=jnp.float32)}
    _L0_ffn_all = _L0_ffn_setup()
    _L0_ffn_in = {k: v for k, v in _L0_ffn_all.items() if k in ('sg', 'su', 'sd', 'rg', 'ru', 'rd', 'wr', 'rb')}
    del _L0_ffn_all
    return {'x': x, 'ctx_1024': ctx_1024, 'g_xattn': g_xattn, 'g_ffn': g_ffn, 'L0_xattn_Wq': _L0_xattn_in['Wq'], 'L0_xattn_bq': _L0_xattn_in['bq'], 'L0_xattn_Wk': _L0_xattn_in['Wk'], 'L0_xattn_bk': _L0_xattn_in['bk'], 'L0_xattn_Wv': _L0_xattn_in['Wv'], 'L0_xattn_bv': _L0_xattn_in['bv'], 'L0_xattn_Wo': _L0_xattn_in['Wo'], 'L0_xattn_bo': _L0_xattn_in['bo'], 'L0_ffn_sg': _L0_ffn_in['sg'], 'L0_ffn_su': _L0_ffn_in['su'], 'L0_ffn_sd': _L0_ffn_in['sd'], 'L0_ffn_rg': _L0_ffn_in['rg'], 'L0_ffn_ru': _L0_ffn_in['ru'], 'L0_ffn_rd': _L0_ffn_in['rd'], 'L0_ffn_wr': _L0_ffn_in['wr'], 'L0_ffn_rb': _L0_ffn_in['rb']}

def reference(x, ctx_1024, g_xattn, g_ffn, L0_xattn_Wq, L0_xattn_bq, L0_xattn_Wk, L0_xattn_bk, L0_xattn_Wv, L0_xattn_bv, L0_xattn_Wo, L0_xattn_bo, L0_ffn_sg, L0_ffn_su, L0_ffn_sd, L0_ffn_rg, L0_ffn_ru, L0_ffn_rd, L0_ffn_wr, L0_ffn_rb):
    import jax
    import jax.numpy as jnp

    def _L0_xattn_ref(queries, keys, values, Wq, bq, Wk, bk, Wv, bv, Wo, bo):
        import jax, jax.numpy as jnp
        import numpy as np
        N_HEADS = 16
        B, L, D = queries.shape
        H = N_HEADS
        dk = D // H

        def split_heads(x):
            return x.reshape(B, L, H, dk).transpose(0, 2, 1, 3)
        q = split_heads(queries @ Wq + bq)
        k = split_heads(keys @ Wk + bk)
        v = split_heads(values @ Wv + bv)
        U = max(1, L // 2)
        q_norm = jnp.linalg.norm(q, axis=-1)
        _, idx = jax.lax.top_k(q_norm, U)
        idx_e = idx[..., None]
        q_s = jnp.take_along_axis(q, idx_e, axis=2)
        k_s = jnp.take_along_axis(k, idx_e, axis=2)
        v_s = jnp.take_along_axis(v, idx_e, axis=2)
        scores = jnp.einsum('bhud,bhwd->bhuw', q_s, k_s) / jnp.sqrt(jnp.float32(dk))
        attn = jax.nn.softmax(scores, axis=-1)
        context = jnp.einsum('bhuw,bhwd->bhud', attn, v_s)
        b_ix = jnp.arange(B)[:, None, None]
        h_ix = jnp.arange(H)[None, :, None]
        full = jnp.zeros((B, H, L, dk), dtype=context.dtype)
        full = full.at[b_ix, h_ix, idx, :].set(context)
        out = full.transpose(0, 2, 1, 3).reshape(B, L, D)
        return out @ Wo + bo

    def _L0_ffn_ref(x, sg, su, sd, rg, ru, rd, wr, rb):
        import jax, jax.numpy as jnp
        import numpy as np
        H, I, E_ROUTED, TOP_K = (128, 352, 7, 2)
        B, S = (4, 256)

        def _expert(h, g, u, d):
            return jnp.einsum('...i,hi->...h', jax.nn.silu(h @ g.T) * (h @ u.T), d)
        shared_out = _expert(x, sg, su, sd)
        logits = x @ wr.T + rb
        probs = jax.nn.softmax(logits, axis=-1)
        scores, idx = jax.lax.top_k(probs, TOP_K)
        scores = scores / scores.sum(axis=-1, keepdims=True)
        w = jnp.sum(scores[..., None] * jax.nn.one_hot(idx, E_ROUTED, dtype=x.dtype), axis=-2)
        out = shared_out
        for e in range(E_ROUTED):
            out = out + w[..., e:e + 1] * _expert(x, rg[e], ru[e], rd[e])
        return out
    x = x + jnp.tanh(g_xattn[0]) * _L0_xattn_ref(_layernorm(x, axis=-1), ctx_1024, ctx_1024, L0_xattn_Wq, L0_xattn_bq, L0_xattn_Wk, L0_xattn_bk, L0_xattn_Wv, L0_xattn_bv, L0_xattn_Wo, L0_xattn_bo)
    x = x + jnp.tanh(g_ffn[0]) * _L0_ffn_ref(_layernorm(x, axis=-1), L0_ffn_sg, L0_ffn_su, L0_ffn_sd, L0_ffn_rg, L0_ffn_ru, L0_ffn_rd, L0_ffn_wr, L0_ffn_rb)
    return x

_drawn_inputs = setup_inputs


def setup_inputs(seed=0):
    import zlib

    import numpy as np

    out = dict(_drawn_inputs(seed))
    spreads = {'L0_xattn_bq': (0.0, 0.1),
     'L0_xattn_bk': (0.0, 0.8),
     'L0_xattn_bv': (0.0, 0.1),
     'L0_xattn_bo': (0.0, 0.1),
     'L0_ffn_rb': (0.0, 0.8)}
    factors = {'L0_ffn_sg': 6.365,
     'L0_ffn_su': 6.19,
     'L0_ffn_sd': 6.239,
     'L0_ffn_rg': 8.0,
     'L0_ffn_ru': 8.0,
     'L0_ffn_rd': 8.0,
     'L0_ffn_wr': 8.0}
    for name, (base, spread) in spreads.items():
        noise = np.random.default_rng([zlib.crc32(name.encode()), seed]).standard_normal(out[name].shape)
        drawn = base * np.exp(spread * noise) if base else spread * noise
        out[name] = jnp.asarray(drawn.astype(out[name].dtype))
    for name, factor in factors.items():
        out[name] = (out[name] * factor).astype(out[name].dtype)
    return out
```

```python
from contextlib import ExitStack

import concourse.bass as bass
from concourse import mybir

F32 = mybir.dt.float32
F32R = mybir.dt.float32r
BF16 = mybir.dt.bfloat16
ALU = mybir.AluOpType
ACT = mybir.ActivationFunctionType
AX = mybir.AxisListType

P = 128
D = 128
B, L = 64, 64
H, DK = 16, 8
U = L // 2
I = 352
E = 8
GB = 8
NG = B // GB
GT = GB * L
NT = GT // P
CH = [(0, 128), (128, 128), (256, 96)]
NC_ = len(CH)
NS = E * NC_
HS = 5
VW = DK + 1
SCORES_AT = {6 + 3 * (b // 2) + b % 2: b for b in range(GB)}
TRANSPOSE_AT = {n + 1: b for n, b in SCORES_AT.items()}
CONTEXT_AT = {9 + 3 * m: m for m in range(NT)}
NORMALISE_AT = {n + 1: m for n, m in CONTEXT_AT.items()}
PROJECT_AT = {n + 2: m for n, m in CONTEXT_AT.items()}
QEXP_AT = {n - 3: b for n, b in SCORES_AT.items()}
BIG = 1e30
EPS = 1e-5
SCALE = float(DK) ** -0.5


def gated_block(nc, x, ctxT, gates, wq, bq, wk, bk, wv, bv, wo, bo, wgu, wd, wrT, rb, out):
    st = ExitStack()
    with st:
        def sb(name, shape, dt=F32):
            return st.enter_context(nc.sbuf_tensor(name, shape, dt))

        def sem(name):
            return st.enter_context(nc.semaphore(name))

        bank = [st.enter_context(nc.psum_tensor(f"bank{i}", [P, 512], F32)) for i in range(8)]

        ident = sb("ident", [P, P])
        quadpick = sb("quadpick", [P, GB, 4, L], BF16)
        picked = sb("picked", [P, GB, 4])
        quadmask = sb("quadmask", [P, 4])
        headsum = sb("headsum", [P, GB, P])
        rowmask = sb("rowmask", [P, 4])
        halfmask = sb("halfmask", [P, 2])
        pick16 = sb("pick16", [16, E, P], F32R)
        firstof = sb("firstof", [P, E - 1])
        negh = sb("negh", [P, NT])
        wq_sb, wk_sb, wv_sb, wo_sb = (sb(n, [P, D]) for n in ("wq_sb", "wk_sb", "wv_sb", "wo_sb"))
        bqk = sb("bqk", [P, 2])
        bv_b = sb("bv_b", [P, D])
        bo_b = sb("bo_b", [P, D])
        tbo = sb("tbo", [P, D])
        rb_b = sb("rb_b", [P, E - 1])
        gate_in = sb("gate_in", [P, 2])
        tgate = sb("tgate", [P, 2])
        wr_sb = sb("wr_sb", [P, 8])
        wr_hi = sb("wr_hi", [P, 8], F32R)
        wr_lo = sb("wr_lo", [P, 8], F32R)
        GUW = E * 2 * I
        gu_hi = sb("gu_hi", [P, GUW], F32R)
        gu_lo = sb("gu_lo", [P, GUW], F32R)
        wd_hi = sb("wd_hi", [P, NC_, E * D], F32R)
        wd_lo = sb("wd_lo", [P, NC_, E * D], F32R)

        xg = sb("xg", [P, NT, D])
        xpb = sb("xpb", [P, NT, D])
        x2 = sb("x2", [P, NT, D])
        ctx = sb("ctx", [P, GB, 2, L])
        stats = sb("stats", [P, NT, 6])
        mv = sb("mv", [P, NT, 2])
        ve = sb("ve", [P, NT])
        rstd = sb("rstd", [P, NT])
        stats2 = sb("stats2", [P, NT, 6])
        mv2 = sb("mv2", [P, NT, 2])
        ve2 = sb("ve2", [P, NT])
        rstd2 = sb("rstd2", [P, NT])
        xn = sb("xn", [P, NT, D])
        xnT = sb("xnT", [P, GT])
        q = sb("q", [P, GT])
        qsq = xnT
        qexp = sb("qexp", [P, GB, 4, L])
        kquad = sb("kquad", [P, 4, GT])
        top8 = sb("top8", [P, 4, 8])
        rest = sb("rest", [P, 4, L])
        keybias = sb("keybias", [P, 4, L], BF16)
        bias = sb("bias", [P, L])
        seld = sb("seld", [P, 2, L])
        selP = sb("selP", [P, NT, H])
        vblk = sb("vblk", [P, GB * 8, 2, VW])
        mx = sb("mx", [P, 2, 8])
        prob = sb("prob", [P, 2, 8, L])
        pick16f = prob[0:16].rearrange("p s a k -> p (s a k)").rearrange("p (e n) -> p e n", e=E)
        probT = sb("probT", [P, 2, 512])
        vtmp = probT[:, 0].rearrange("p (b d) -> p b d", b=4)
        rec = sb("rec", [P, 2, H])
        recs = sb("recs", [P, 2, H])
        cn = sb("cn", [P, 2, D])
        cnT = sb("cnT", [P, 2, D])
        xn2 = xn
        xhi = sb("xhi", [P, GT], F32R)
        xlo = sb("xlo", [P, GT], F32R)
        lg = sb("lg", [P, NT, 7])
        lt = sb("lt", [P, NT, 7])
        oh1 = sb("oh1", [P, NT, 7])
        oh2 = sb("oh2", [P, NT, 7])
        rs = sb("rs", [P, 8, NT])
        W = sb("W", [P, NT, 8])
        W16 = sb("W16", [P, NT, 16])
        whi = sb("whi", [P, NT, 8], F32R)
        WT = sb("WT", [16, GT], F32R)
        work = sb("work", [P, 7168])
        wB = work[:, 0:1024].rearrange("p (s t) -> p s t", s=2)
        acc = work[:, 1024:1536]
        yw = work[:, 1536:2048]
        fin = work[:, 2048:2560].rearrange("p (m d) -> p m d", m=NT)
        x2keep = work[:, 2560:3072].rearrange("p (m d) -> p m d", m=NT)
        tg = work[:, 4096:5120].rearrange("p (s t) -> p s t", s=2)
        ag = work[:, 5120:6144].rearrange("p (s t) -> p s t", s=2)
        hg = work[:, 6144:7168].rearrange("p (s t) -> p s t", s=2)
        h_hi = sb("h_hi", [P, HS, GT], F32R)
        h_lo = sb("h_lo", [P, HS, GT], F32R)

        small_in = sem("small_in")
        wqkv_in = sem("wqkv_in")
        wgt_a_in = sem("wgt_a_in")
        wgt_b_in = sem("wgt_b_in")
        wgt_c_in = sem("wgt_c_in")
        wgt_c2_in = sem("wgt_c2_in")
        c_ident = sem("c_ident")
        c_gp = sem("c_gp")
        c_masks = sem("c_masks")
        c_zero = sem("c_zero")
        c_pick = sem("c_pick")
        rowmask_ok = sem("rowmask_ok")
        pick_ok = sem("pick_ok")
        tgate_ok = sem("tgate_ok")
        tbo_ok = sem("tbo_ok")
        wr_ok = sem("wr_ok")
        wgt_hi = sem("wgt_hi")
        wgt_lo = sem("wgt_lo")
        wgt_c_hi = sem("wgt_c_hi")
        wgt_c_lo = sem("wgt_c_lo")
        x_in = sem("x_in")
        ctx_in = sem("ctx_in")
        out_done = sem("out_done")
        bn_ok = sem("bn_ok")
        mv_ok = sem("mv_ok")
        var_ok = sem("var_ok")
        rstd_ok = sem("rstd_ok")
        xn_ok = sem("xn_ok")
        xpb_ok = sem("xpb_ok")
        xnT_ps = sem("xnT_ps")
        xnT_ok = sem("xnT_ok")
        q_ps = sem("q_ps")
        k_ps = sem("k_ps")
        q_ok = sem("q_ok")
        k_ok = sem("k_ok")
        qsq_ok = sem("qsq_ok")
        qexp_ok = sem("qexp_ok")
        norm_ps = sem("norm_ps")
        top_ok = sem("top_ok")
        bias_ok = sem("bias_ok")
        mask_ok = sem("mask_ok")
        seld_ok = sem("seld_ok")
        selT_ps = sem("selT_ps")
        selP_ok = sem("selP_ok")
        v_ps = sem("v_ps")
        vtmp_ok = sem("vtmp_ok")
        vblk_ok = sem("vblk_ok")
        s_ps = sem("s_ps")
        mx_ok = sem("mx_ok")
        sub_ok = sem("sub_ok")
        exp_ok = sem("exp_ok")
        pT_ps = sem("pT_ps")
        pT_ok = sem("pT_ok")
        pv_ps = sem("pv_ps")
        rec_ok = sem("rec_ok")
        recs_ok = sem("recs_ok")
        cn_ok = sem("cn_ok")
        cT_ps = sem("cT_ps")
        cT_ok = sem("cT_ok")
        o_ps = sem("o_ps")
        x2_ok = sem("x2_ok")
        bn2_ok = sem("bn2_ok")
        mv2_ok = sem("mv2_ok")
        var2_ok = sem("var2_ok")
        rstd2_ok = sem("rstd2_ok")
        xn2_ok = sem("xn2_ok")
        xn2T_ps = sem("xn2T_ps")
        xhi_ok = sem("xhi_ok")
        xlo_ok = sem("xlo_ok")
        lg_ps = sem("lg_ps")
        lg_ok = sem("lg_ok")
        rt_ok = sem("rt_ok")
        dif_ok = sem("dif_ok")
        edif_ok = sem("edif_ok")
        w_ok = sem("w_ok")
        var_w = sem("var_w")
        wT_ps = sem("wT_ps")
        wT_ok = sem("wT_ok")
        wB_ps = sem("wB_ps")
        wB_ok = sem("wB_ok")
        g_ps = sem("g_ps")
        u_ps = sem("u_ps")
        t_ok = sem("t_ok")
        a_ok = sem("a_ok")
        h_ok = sem("h_ok")
        hi_ok = sem("hi_ok")
        lo_ok = sem("lo_ok")
        y_ps = sem("y_ps")
        yw_ok = sem("yw_ok")
        acc_ok = sem("acc_ok")
        fT_ps = sem("fT_ps")
        keep_ok = sem("keep_ok")
        fin_ok = sem("fin_ok")

        arrived = sem("arrived")
        go = {e.engine: sem(f"go_{n}") for n, e in (("sync", nc.sync), ("scalar", nc.scalar), ("vector", nc.vector),
                                                     ("tensor", nc.tensor))}

        block = st.enter_context(nc.Block())
        counted = range(x_in.num, fin_ok.num + 1)

        def meet(eng):
            eng.drain().then_inc(arrived, 1)
            eng.wait_ge(go[eng.engine], 1)
            eng.sem_inc(go[eng.engine], -1)

        def meet_pool(gp):
            gp.drain()
            gp.wait_ge(arrived, 4)
            gp.sem_inc(arrived, -4)
            gp.sem_clear(counted)
            for sem_ in go.values():
                gp.sem_inc(sem_, 1)

        x_v = x.rearrange("(t p) d -> p t d", p=P)
        out_v = out.rearrange("(t p) d -> p t d", p=P)

        @block.sync
        def _(sp):
            def load_x(g):
                sp.dma_start(xg[:], x_v[:, bass.ds(g * NT, NT), :]).then_inc(x_in, 16)

            def load_ctx(g):
                src = ctxT[:, bass.ds(g * GT, GT)].rearrange("p (b l) -> p b l", b=GB)
                for twice in range(2):
                    sp.dma_start(ctx[:, :, twice], src).then_inc(ctx_in, 16)

            def next_group(g):
                sp.wait_ge(xn_ok, 1)
                sp.wait_ge(xpb_ok, 1)
                load_x(g)
                sp.wait_ge(k_ps, 1)
                sp.wait_ge(v_ps, 2)
                load_ctx(g)

            def store(g):
                sp.wait_ge(fin_ok, 1)
                sp.dma_start(out_v[:, bass.ds(g * NT, NT), :], fin).then_inc(out_done, 16)

            def landed():
                sp.wait_ge(x_in, 16)
                sp.wait_ge(ctx_in, 32)

            load_x(0)
            for dst, src in ((wq_sb, wq), (wk_sb, wk), (wv_sb, wv), (wo_sb, wo)):
                sp.dma_start(dst[:], src).then_inc(wqkv_in, 16)
            load_ctx(0)
            for dst, src in ((bqk[:, 0:1], bq.unsqueeze(1)), (bqk[:, 1:2], bk.unsqueeze(1)),
                             (wr_sb[:, 0:7], wrT),
                             (bv_b[:], bv.unsqueeze(0).broadcast_to([P, D])),
                             (bo_b[:], bo.unsqueeze(0).broadcast_to([P, D])),
                             (rb_b[:], rb.unsqueeze(0).broadcast_to([P, 7])),
                             (gate_in[:], gates.unsqueeze(0).broadcast_to([P, 2]))):
                sp.dma_start(dst, src).then_inc(small_in, 16)
            half = GUW // 2
            sp.dma_start(work[:, 0:half], wgu[:, 0:half]).then_inc(wgt_a_in, 16)
            sp.dma_start(work[:, half:GUW], wgu[:, half:GUW]).then_inc(wgt_b_in, 16)
            sp.dma_start(work[0:96, GUW:GUW + E * D].rearrange("p (e h) -> p e h", e=E),
                         wd[:, 256:352, :].rearrange("e i h -> i e h")).then_inc(wgt_c2_in, 16)
            next_group(1)
            sp.wait_ge(wgt_hi, 1)
            sp.wait_ge(wgt_lo, 1)
            for c in range(2):
                sp.dma_start(work[:, c * E * D:(c + 1) * E * D].rearrange("p (e h) -> p e h", e=E),
                             wd[:, c * P:(c + 1) * P, :].rearrange("e i h -> i e h")).then_inc(wgt_c_in, 16)
            sp.wait_ge(x_in, 32)
            sp.wait_ge(ctx_in, 64)
            meet(sp)
            next_group(2)
            landed()
            meet(sp)
            with sp.Fori(2, NG - 1) as g:
                store(g - 2)
                next_group(g + 1)
                landed()
                sp.wait_ge(out_done, 16)
                meet(sp)
            store(NG - 3)
            sp.wait_ge(out_done, 16)
            meet(sp)
            store(NG - 2)
            sp.wait_ge(fin_ok, 2)
            sp.dma_start(out_v[:, (NG - 1) * NT:NG * NT, :], fin).then_inc(out_done, 16)
            sp.wait_ge(out_done, 32)

        @block.gpsimd
        def _(gp):
            gp.memset(ident[:], 0.0).then_inc(c_gp, 1)
            gp.memset(headsum[:], 1.0).then_inc(c_gp, 1)
            gp.memset(pick16f, 0.0).then_inc(c_gp, 1)
            gp.memset(wr_sb[:, 7:8], 0.0).then_inc(c_gp, 1)
            gp.memset(negh[:], -0.5).then_inc(c_gp, 1)
            for e in range(E - 1):
                gp.memset(firstof[:, e:e + 1], float(7 - e)).then_inc(c_gp, 1)
            gp.wait_ge(c_gp, 12)
            gp.affine_select(out=ident[:], in_=ident[:], compare_op=ALU.not_equal, fill=1.0, base=0,
                             pattern=[[-1, P]], channel_multiplier=1).then_inc(c_ident, 1)
            gp.affine_select(out=headsum[:], in_=headsum[:], compare_op=ALU.is_ge, fill=0.0, base=0,
                             pattern=[[P, GB], [-DK, P]], channel_multiplier=1).then_inc(c_gp, 1)
            gp.affine_select(out=pick16f, in_=pick16f, compare_op=ALU.not_equal, fill=1.0, base=0,
                             pattern=[[-1, E], [0, P]], channel_multiplier=1).then_inc(c_gp, 1)
            gp.wait_ge(c_gp, 14)
            gp.affine_select(out=headsum[:], in_=headsum[:], compare_op=ALU.is_ge, fill=0.0, base=DK - 1,
                             pattern=[[-P, GB], [DK, P]], channel_multiplier=-1).then_inc(c_masks, 1)
            gp.affine_select(out=pick16f, in_=pick16f, compare_op=ALU.not_equal, fill=1.0, base=-E,
                             pattern=[[-1, E], [0, P]], channel_multiplier=1).then_inc(c_pick, 1)

            def expand_queries(b):
                gp.tensor_tensor(
                    qexp[:, b], q[:, b * L:(b + 1) * L].unsqueeze(1).broadcast_to([P, 4, L]),
                    rowmask[:].unsqueeze(2).broadcast_to([P, 4, L]), ALU.mult).then_inc(qexp_ok, 1)

            def spread_values(hv):
                gp.wait_ge(vtmp_ok, hv + 1)
                for px in range(2):
                    src = vtmp.rearrange("p b (j x c d) -> p (b j) x c d", j=4, x=2, c=2)[:, :, px]
                    dst = vblk[:, hv * 32:hv * 32 + 32, px, 0:DK].rearrange("p (n c) d -> p n c d", c=2)
                    gp.tensor_scalar(dst, src, halfmask[:, px:px + 1], None, ALU.mult).then_inc(vblk_ok, 1)

            def attend(n):
                if n == 0:
                    gp.wait_ge(var_ok, 1)
                    gp.tensor_tensor(rstd[:], ve[:], negh[:], ALU.pow).then_inc(rstd_ok, 1)
                if n == 1:
                    gp.wait_ge(tbo_ok, 1)
                    gp.tensor_tensor(xpb[:], xg[:], tbo[:].unsqueeze(1).broadcast_to([P, NT, D]),
                                     ALU.add).then_inc(xpb_ok, 1)
                if n == 2:
                    gp.wait_ge(q_ok, 1)
                    gp.tensor_tensor(qsq[:], q[:], q[:], ALU.mult).then_inc(qsq_ok, 1)
                    gp.wait_ge(rowmask_ok, 1)
                    gp.wait_ge(c_zero, 8)
                if n in QEXP_AT:
                    expand_queries(QEXP_AT[n])
                if n == 5:
                    spread_values(0)
                if n == 7:
                    spread_values(1)
                if n == 21:
                    gp.wait_ge(var2_ok, 1)
                    gp.tensor_tensor(rstd2[:], ve2[:], negh[:], ALU.pow).then_inc(rstd2_ok, 1)

            def weights_lo():
                half = GUW // 2
                for k in range(2):
                    gp.wait_ge(wgt_hi, k + 1)
                    gp.tensor_tensor(gu_lo[:, k * half:(k + 1) * half], work[:, k * half:(k + 1) * half],
                                     gu_hi[:, k * half:(k + 1) * half].bitcast(F32),
                                     ALU.subtract).then_inc(wgt_lo, 1)
                gp.wait_ge(wgt_c_hi, 1)
                gp.tensor_tensor(wd_lo[0:96, 2], work[0:96, GUW:GUW + E * D], wd_hi[0:96, 2].bitcast(F32),
                                 ALU.subtract).then_inc(wgt_c_lo, 1)
                for c in range(2):
                    gp.wait_ge(wgt_c_hi, c + 2)
                    gp.tensor_tensor(wd_lo[:, c], work[:, c * E * D:(c + 1) * E * D],
                                     wd_hi[:, c].bitcast(F32), ALU.subtract).then_inc(wgt_c_lo, 1)

            def lo_part(n):
                w = CH[n % 3][1]
                gp.wait_ge(hi_ok, n + 1)
                gp.tensor_tensor(h_lo[0:w, n % HS], hg[0:w, n % 2], h_hi[0:w, n % HS].bitcast(F32),
                                 ALU.subtract).then_inc(lo_ok, 1)

            def add_expert(e):
                gp.wait_ge(yw_ok, e + 1)
                if e == 0:
                    gp.tensor_copy(acc, yw).then_inc(acc_ok, 1)
                else:
                    gp.wait_ge(acc_ok, e)
                    gp.tensor_tensor(acc, acc, yw, ALU.add).then_inc(acc_ok, 1)

            def iteration(experts, attention):
                for n in range(NS):
                    if attention and n == 0:
                        attend(0)
                    if experts and n >= 1:
                        lo_part(n - 1)
                    if experts and n % 3 == 2 and n >= 5:
                        add_expert((n - 5) // 3)
                    if attention and n > 0:
                        attend(n)
                if experts:
                    lo_part(NS - 1)
                    add_expert(E - 1)

            iteration(False, True)
            weights_lo()
            meet_pool(gp)
            iteration(True, True)
            meet_pool(gp)
            with gp.Fori(2, NG):
                iteration(True, True)
                meet_pool(gp)
            iteration(True, False)

        @block.scalar
        def _(act):
            act.wait_ge(small_in, 16 * 7)
            act.activation(tgate[:], gate_in[:], ACT.Tanh).then_inc(tgate_ok, 1)

            def weights_hi():
                half = GUW // 2
                for k, arrived in enumerate((wgt_a_in, wgt_b_in)):
                    act.wait_ge(arrived, 16)
                    act.copy(gu_hi[:, k * half:(k + 1) * half],
                             work[:, k * half:(k + 1) * half]).then_inc(wgt_hi, 1)
                act.wait_ge(wgt_c2_in, 16)
                act.copy(wd_hi[0:96, 2], work[0:96, GUW:GUW + E * D]).then_inc(wgt_c_hi, 1)
                act.wait_ge(wgt_c_in, 32)
                for c in range(2):
                    act.copy(wd_hi[:, c], work[:, c * E * D:(c + 1) * E * D]).then_inc(wgt_c_hi, 1)

            def probT_copy(b):
                act.wait_ge(pT_ps, b + 1)
                if b == 0:
                    act.wait_ge(vblk_ok, 4)
                if b >= 2:
                    act.wait_ge(pv_ps, b - 1)
                act.copy(probT[:, b % 2], bank[6][:]).then_inc(pT_ok, 1)

            def ctx_copy(m):
                act.wait_ge(cT_ps, m + 1)
                if m >= 2:
                    act.wait_ge(o_ps, m - 1)
                act.copy(cnT[:, m % 2], bank[7][:, 0:D]).then_inc(cT_ok, 1)

            def round_h(n):
                w = CH[n % 3][1]
                act.wait_ge(h_ok, n + 1)
                if n >= HS:
                    act.wait_ge(y_ps, (n - HS) // 3 + 1)
                act.copy(h_hi[0:w, n % HS], hg[0:w, n % 2]).then_inc(hi_ok, 1)

            def gate_tanh(n):
                w = CH[n % 3][1]
                act.wait_ge(g_ps, n + 1)
                if n >= 2:
                    act.wait_ge(a_ok, n - 1)
                act.activation(tg[0:w, n % 2], bank[n % 2][0:w, :], ACT.Tanh, scale=0.5).then_inc(t_ok, 1)

            def weight_copy(e):
                act.wait_ge(wB_ps, e + 1)
                act.copy(wB[:, e % 2], bank[4][:]).then_inc(wB_ok, 1)

            def attend(n):
                if n == 1:
                    act.wait_ge(xnT_ps, 1)
                    act.copy(xnT[:], bank[5][:]).then_inc(xnT_ok, 1)
                if n == 2:
                    act.wait_ge(q_ps, 1)
                    act.activation(q[:], bank[6][:], ACT.Identity, bias=bqk[:, 0:1]).then_inc(q_ok, 1)
                    act.wait_ge(c_zero, 1)
                    for j in range(4):
                        r = slice(32 * j, 32 * j + 32)
                        act.activation(kquad[r, j], bank[7][r, :], ACT.Identity,
                                       bias=bqk[r, 1:2]).then_inc(k_ok, 1)

            def exponentials(b):
                act.wait_ge(sub_ok, b + 1)
                act.activation(prob[:, b % 2], prob[:, b % 2], ACT.Exp, scale=SCALE).then_inc(exp_ok, 1)

            def iteration(experts, attention):
                for n in range(NS):
                    if attention and n - 1 in TRANSPOSE_AT:
                        probT_copy(TRANSPOSE_AT[n - 1])
                    if attention and n in PROJECT_AT:
                        ctx_copy(PROJECT_AT[n])
                    if experts:
                        gate_tanh(n)
                    if attention and n in TRANSPOSE_AT:
                        exponentials(TRANSPOSE_AT[n])
                    if experts:
                        if n >= 1:
                            round_h(n - 1)
                        if n == 2:
                            act.wait_ge(wT_ps, 1)
                            act.copy(WT[:], bank[4][0:16, :]).then_inc(wT_ok, 1)
                        if n == 1:
                            act.wait_ge(dif_ok, 1)
                            act.activation(rs[:, 3], rs[:, 2], ACT.Exp).then_inc(edif_ok, 1)
                        if n % 3 == 0 and n >= 3:
                            weight_copy(n // 3 - 1)
                    if attention:
                        attend(n)
                if experts:
                    weight_copy(E - 1)
                    round_h(NS - 1)
                if attention:
                    act.wait_ge(xn2T_ps, 1)
                    if experts:
                        act.wait_ge(u_ps, NS)
                    act.copy(xhi[:], bank[6][:]).then_inc(xhi_ok, 1)

            iteration(False, True)
            weights_hi()
            meet(act)
            iteration(True, True)
            meet(act)
            with act.Fori(2, NG):
                iteration(True, True)
                meet(act)
            iteration(True, False)

        @block.vector
        def _(dve):
            dve.memset(kquad[:], 0.0).then_inc(c_zero, 1)
            dve.memset(vblk[:], 0.0).then_inc(c_zero, 1)
            dve.memset(W[:], 0.5).then_inc(c_zero, 1)
            dve.memset(halfmask[:], 0.0).then_inc(c_zero, 1)
            dve.wait_ge(c_zero, 4)
            dve.memset(halfmask[0:64, 0:1], 1.0).then_inc(c_zero, 1)
            dve.memset(halfmask[64:128, 1:2], 1.0).then_inc(c_zero, 1)
            dve.memset(vblk[0:64, :, 0, DK:VW], 1.0).then_inc(c_zero, 1)
            dve.memset(vblk[64:128, :, 1, DK:VW], 1.0).then_inc(c_zero, 1)
            dve.wait_ge(c_ident, 1)
            dve.tensor_reduce(picked[:], ident[:].rearrange("p (b j r) -> p b r j", b=GB, j=4), AX.X,
                              ALU.add).then_inc(c_zero, 1)
            dve.tensor_reduce(quadmask[:], ident[:].rearrange("p (b j r) -> p j b r", b=GB, j=4), AX.XY,
                              ALU.add).then_inc(c_zero, 1)
            dve.wait_ge(c_zero, 10)
            dve.tensor_copy(quadpick[:], picked[:].unsqueeze(3).broadcast_to([P, GB, 4, L])).then_inc(c_zero, 1)
            dve.wait_ge(c_masks, 1)
            dve.tensor_reduce(rowmask[:], headsum[:, 0, 0:H].rearrange("p (j r) -> p r j", r=4), AX.X,
                              ALU.add).then_inc(rowmask_ok, 1)
            dve.wait_ge(c_pick, 1)
            dve.tensor_copy(pick16[:], pick16f).then_inc(pick_ok, 1)

            def first_norm():
                for m in range(NT):
                    i = dve.bn_stats(stats[:, m], xg[:, m])
                i.then_inc(bn_ok, 1)
                dve.wait_ge(bn_ok, 1)
                for m in range(NT):
                    i = dve.bn_aggr(mv[:, m], stats[:, m])
                i.then_inc(mv_ok, 1)
                dve.wait_ge(mv_ok, 1)
                dve.tensor_scalar(ve[:], mv[:, :, 1], EPS, None, ALU.add).then_inc(var_ok, 1)
                dve.wait_ge(rstd_ok, 1)
                for m in range(NT):
                    i = dve.tensor_scalar(xn[:, m], xg[:, m], mv[:, m, 0:1], rstd[:, m:m + 1],
                                          ALU.subtract, ALU.mult)
                i.then_inc(xn_ok, 1)

            def once():
                dve.wait_ge(small_in, 16 * 7)
                dve.wait_ge(tgate_ok, 1)
                dve.tensor_scalar(tbo[:], bo_b[:], tgate[:, 0:1], None, ALU.mult).then_inc(tbo_ok, 1)
                dve.wait_ge(c_gp, 4)
                dve.tensor_copy(wr_hi[:], wr_sb[:]).then_inc(wr_ok, 1)
                dve.wait_ge(wr_ok, 1)
                dve.tensor_tensor(wr_lo[:], wr_sb[:], wr_hi[:].bitcast(F32), ALU.subtract).then_inc(wr_ok, 1)

            def choose():
                dve.wait_ge(norm_ps, 1)
                src = bank[5][:, 0:L]
                for r in range(4):
                    dve.max(top8[:, r], src).then_inc(top_ok, 1)
                    dve.wait_ge(top_ok, 2 * r + 1)
                    dve.match_replace(rest[:, r], top8[:, r], src, -1.0).then_inc(top_ok, 1)
                    dve.wait_ge(top_ok, 2 * r + 2)
                    src = rest[:, r]
                dve.tensor_scalar(bias[:], src, 0.0, -BIG, ALU.is_ge, ALU.mult).then_inc(bias_ok, 1)
                dve.tensor_scalar(seld[:], src.unsqueeze(1).broadcast_to([P, 2, L]), 0.0, None,
                                  ALU.is_lt).then_inc(seld_ok, 1)
                dve.wait_ge(bias_ok, 1)
                dve.tensor_tensor(keybias[:], bias[:].unsqueeze(1).broadcast_to([P, 4, L]),
                                  quadmask[:].unsqueeze(2).broadcast_to([P, 4, L]), ALU.mult).then_inc(mask_ok, 1)

            def value_bias(hv):
                dve.wait_ge(v_ps, hv + 1)
                if hv:
                    dve.wait_ge(vblk_ok, 2)
                dve.tensor_tensor(vtmp, bank[7][:].rearrange("p (b d) -> p b d", b=4),
                                  bv_b[:].unsqueeze(1).broadcast_to([P, 4, D]), ALU.add).then_inc(vtmp_ok, 1)

            def query_mask():
                dve.wait_ge(selT_ps, 1)
                sT = bank[6][:, 0:P].rearrange("p (m x h) -> p m x h", m=NT, x=2)
                dve.tensor_copy(selP[0:64], sT[0:64, :, 0]).then_inc(selP_ok, 1)
                dve.tensor_copy(selP[64:128], sT[64:128, :, 1]).then_inc(selP_ok, 1)

            def normalise(m):
                dve.wait_ge(pv_ps, 2 * m + 2)
                c = bank[7][:, 0:H * VW].rearrange("p (n v) -> p n v", v=VW)
                dve.reciprocal(rec[:, m % 2], c[:, :, DK]).then_inc(rec_ok, 1)
                dve.wait_ge(rec_ok, m + 1)
                dve.wait_ge(selP_ok, 2)
                dve.tensor_tensor(recs[:, m % 2].rearrange("p (j c x) -> p j c x", j=4, c=2),
                                  rec[:, m % 2].rearrange("p (j c x) -> p j c x", j=4, c=2),
                                  selP[:, m].rearrange("p (j x c) -> p j c x", j=4, x=2),
                                  ALU.mult).then_inc(recs_ok, 1)
                dve.wait_ge(recs_ok, m + 1)
                if m >= 2:
                    dve.wait_ge(cT_ps, m - 1)
                dve.tensor_tensor(cn[:, m % 2].rearrange("p (n d) -> p n d", d=DK), c[:, :, 0:DK],
                                  recs[:, m % 2].unsqueeze(2).broadcast_to([P, H, DK]),
                                  ALU.mult).then_inc(cn_ok, 1)

            def residual(m):
                dve.wait_ge(o_ps, m + 1)
                dve.wait_ge(xpb_ok, 1)
                dve.scalar_tensor_tensor(x2[:, m], bank[7][:, 0:D], tgate[:, 0:1], xpb[:, m],
                                         ALU.mult, ALU.add).then_inc(x2_ok, 1)
                dve.wait_ge(x2_ok, m + 1)
                dve.bn_stats(stats2[:, m], x2[:, m]).then_inc(bn2_ok, 1)
                dve.wait_ge(bn2_ok, m + 1)
                dve.bn_aggr(mv2[:, m], stats2[:, m]).then_inc(mv2_ok, 1)

            def softmax_shift(b):
                sc = bank[5][:].rearrange("p (n k) -> p n k", n=8)
                dve.wait_ge(s_ps, b + 1)
                dve.tensor_reduce(mx[:, b % 2], sc, AX.X, ALU.max).then_inc(mx_ok, 1)
                dve.wait_ge(mx_ok, b + 1)
                if b >= 2:
                    dve.wait_ge(pT_ps, b - 1)
                dve.tensor_tensor(prob[:, b % 2], sc, mx[:, b % 2].unsqueeze(2).broadcast_to([P, 8, L]),
                                  ALU.subtract).then_inc(sub_ok, 1)

            def second_var():
                dve.wait_ge(mv2_ok, NT)
                dve.tensor_scalar(ve2[:], mv2[:, :, 1], EPS, None, ALU.add).then_inc(var2_ok, 1)

            def second_norm():
                dve.wait_ge(rstd2_ok, 1)
                for m in range(NT):
                    i = dve.tensor_scalar(xn2[:, m], x2[:, m], mv2[:, m, 0:1], rstd2[:, m:m + 1],
                                          ALU.subtract, ALU.mult)
                i.then_inc(xn2_ok, 1)

            def take_logits():
                dve.tensor_tensor(lg[:], bank[7][:, 0:NT * 8].rearrange("p (m e) -> p m e", e=8)[:, :, 0:7],
                                  rb_b[:].unsqueeze(1).broadcast_to([P, NT, 7]), ALU.add).then_inc(lg_ok, 1)

            def top2():
                k = [0]

                def step(ins):
                    k[0] += 1
                    ins.then_inc(rt_ok, 1)
                    dve.wait_ge(rt_ok, k[0])

                b7 = lambda a: a.unsqueeze(2).broadcast_to([P, NT, 7])
                first = firstof[:].unsqueeze(1).broadcast_to([P, NT, 7])
                m1, m2, dif, edif, den, w1, w2, v = (rs[:, i] for i in range(8))
                dve.wait_ge(lg_ok, 1)
                for top, pick in ((m1, oh1), (m2, oh2)):
                    step(dve.tensor_reduce(top, lg[:], AX.X, ALU.max))
                    step(dve.tensor_tensor(lt[:], lg[:], b7(top), ALU.is_equal))
                    step(dve.tensor_tensor(lt[:], lt[:], first, ALU.mult))
                    step(dve.tensor_reduce(v, lt[:], AX.X, ALU.max))
                    step(dve.tensor_tensor(pick[:], lt[:], b7(v), ALU.is_equal))
                    if pick is oh1:
                        dve.scalar_tensor_tensor(lg[:], oh1[:], -BIG, lg[:], ALU.mult, ALU.add).then_inc(w_ok, 1)
                        dve.wait_ge(w_ok, 1)
                dve.tensor_tensor(dif, m2, m1, ALU.subtract).then_inc(dif_ok, 1)
                dve.wait_ge(edif_ok, 1)
                dve.tensor_scalar(den, edif, 1.0, 2.0, ALU.add, ALU.mult).then_inc(w_ok, 1)
                dve.wait_ge(w_ok, 2)
                dve.reciprocal(w1, den).then_inc(w_ok, 1)
                dve.wait_ge(w_ok, 3)
                dve.tensor_tensor(w2, edif, w1, ALU.mult).then_inc(w_ok, 1)
                dve.tensor_tensor(oh1[:], oh1[:], b7(w1), ALU.mult).then_inc(w_ok, 1)
                dve.wait_ge(w_ok, 5)
                dve.tensor_tensor(oh2[:], oh2[:], b7(w2), ALU.mult).then_inc(w_ok, 1)
                dve.wait_ge(w_ok, 6)
                dve.tensor_tensor(W[:, :, 1:8], oh1[:], oh2[:], ALU.add).then_inc(w_ok, 1)
                dve.wait_ge(w_ok, 7)
                dve.tensor_copy(whi[:], W[:]).then_inc(w_ok, 1)
                dve.wait_ge(w_ok, 8)
                dve.tensor_copy(W16[:, :, 0:8], whi[:].bitcast(F32))
                dve.tensor_tensor(W16[:, :, 8:16], W[:], whi[:].bitcast(F32), ALU.subtract).then_inc(var_w, 1)

            def weigh(e):
                dve.wait_ge(y_ps, e + 1)
                dve.wait_ge(wB_ok, e + 1)
                if e >= 1:
                    dve.wait_ge(acc_ok, e)
                dve.tensor_tensor(yw, bank[4][:], wB[:, e % 2], ALU.mult).then_inc(yw_ok, 1)

            def hidden(n):
                w = CH[n % 3][1]
                dve.wait_ge(t_ok, n + 1)
                dve.scalar_tensor_tensor(ag[0:w, n % 2], tg[0:w, n % 2], 1.0, bank[n % 2][0:w, :],
                                         ALU.add, ALU.mult).then_inc(a_ok, 1)
                dve.wait_ge(a_ok, n + 1)
                dve.wait_ge(u_ps, n + 1)
                if n >= 2:
                    dve.wait_ge(lo_ok, n - 1)
                dve.tensor_tensor(hg[0:w, n % 2], ag[0:w, n % 2], bank[2 + n % 2][0:w, :],
                                  ALU.mult).then_inc(h_ok, 1)

            def finish(k):
                dve.wait_ge(fT_ps, k)
                if k > 1:
                    dve.wait_ge(keep_ok, 1)
                    dve.wait_ge(out_done, 16)
                dve.scalar_tensor_tensor(fin, bank[4][:].rearrange("p (m d) -> p m d", m=NT), tgate[:, 1:2],
                                         x2keep, ALU.mult, ALU.add).then_inc(fin_ok, 1)

            def attend(n):
                if n == 3:
                    choose()
                if n == 4:
                    value_bias(0)
                if n == 5:
                    query_mask()
                if n == 6:
                    value_bias(1)
                if n in SCORES_AT:
                    softmax_shift(SCORES_AT[n])
                if n in PROJECT_AT:
                    residual(PROJECT_AT[n])
                if n == 20:
                    second_var()
                if n == 21:
                    second_norm()

            def iteration(experts, attention, finishing):
                if experts:
                    take_logits()
                for n in range(NS):
                    if attention and n == 0:
                        first_norm()
                    if attention and n in NORMALISE_AT:
                        normalise(NORMALISE_AT[n])
                    if experts:
                        hidden(n)
                        if n == 0:
                            if finishing:
                                finish(1)
                                dve.wait_ge(fin_ok, 1)
                            dve.tensor_copy(x2keep, x2[:]).then_inc(keep_ok, 1)
                            top2()
                        if n % 3 == 2 and n >= 5:
                            weigh((n - 5) // 3)
                    if attention:
                        attend(n)
                if attention:
                    dve.wait_ge(xhi_ok, 1)
                    dve.tensor_tensor(xlo[:], bank[6][:], xhi[:].bitcast(F32), ALU.subtract).then_inc(xlo_ok, 1)
                if experts:
                    weigh(E - 1)

            once()
            dve.wait_ge(x_in, 16)
            iteration(False, True, False)
            meet(dve)
            iteration(True, True, False)
            meet(dve)
            with dve.Fori(2, NG):
                iteration(True, True, True)
                meet(dve)
            iteration(True, False, True)
            finish(2)

        @block.tensor
        def _(pe):
            def values(hv):
                if hv:
                    pe.wait_ge(vtmp_ok, 1)
                else:
                    pe.wait_ge(k_ok, 4)
                for b in range(4):
                    i = pe.matmul(bank[7][:, b * D:(b + 1) * D],
                                  ctx[:, hv * 4 + b].rearrange("p a l -> p (a l)"), wv_sb[:],
                                  start=True, stop=True)
                i.then_inc(v_ps, 1)

            def scores(b):
                pe.wait_ge(qexp_ok, b + 1)
                if b == 0:
                    pe.wait_ge(mask_ok, 1)
                else:
                    pe.wait_ge(sub_ok, b)
                for pp in range(2):
                    dst = bank[5][:].rearrange("p (j x k) -> p j x k", j=4, x=2)[:, :, pp]
                    pair = slice(2 * pp, 2 * pp + 2)
                    pe.matmul(dst, qexp[:, b, pair], kquad[:, :, b * L:(b + 1) * L],
                              start=True, stop=False)
                    i = pe.matmul(dst, quadpick[:, b, pair].rearrange("p a l -> p (a l)"),
                                  keybias[:], start=False, stop=True)
                i.then_inc(s_ps, 1)

            def prob_transposes(b):
                pe.wait_ge(exp_ok, b + 1)
                if b == 0:
                    pe.wait_ge(selP_ok, 2)
                else:
                    pe.wait_ge(pT_ok, b)
                for j in range(4):
                    i = pe.transpose(bank[6][:, j * P:(j + 1) * P],
                                     prob[:, b % 2, 2 * j:2 * j + 2].rearrange("p a k -> p (a k)"), ident[:])
                i.then_inc(pT_ps, 1)

            def context(b):
                pe.wait_ge(pT_ok, b + 1)
                pe.wait_ge(vblk_ok, 2 * (b // 4) + 2)
                if b == 0:
                    pe.wait_ge(vtmp_ok, 2)
                elif b % 2 == 0:
                    pe.wait_ge(x2_ok, b // 2)
                r = slice(64 * (b % 2), 64 * (b % 2) + 64)
                for n in range(8):
                    i = pe.matmul(bank[7][r, n * 2 * VW:(n + 1) * 2 * VW], probT[:, b % 2, n * 64:(n + 1) * 64],
                                  vblk[:, b * 8 + n].rearrange("p x v -> p (x v)"), start=True, stop=True)
                i.then_inc(pv_ps, 1)

            def ctx_transpose(m):
                pe.wait_ge(cn_ok, m + 1)
                pe.transpose(bank[7][:, 0:D], cn[:, m % 2], ident[:]).then_inc(cT_ps, 1)

            def project(m):
                pe.wait_ge(cT_ok, m + 1)
                pe.matmul(bank[7][:, 0:D], cnT[:, m % 2], wo_sb[:], start=True, stop=True).then_inc(o_ps, 1)

            def second_transposes():
                pe.wait_ge(xn2_ok, 1)
                pe.wait_ge(pT_ok, GB)
                for m in range(NT):
                    i = pe.transpose(bank[6][:, m * P:(m + 1) * P], xn2[:, m], ident[:])
                i.then_inc(xn2T_ps, 1)

            def logits():
                pe.wait_ge(xlo_ok, 1)
                for m in range(NT):
                    t = slice(m * P, (m + 1) * P)
                    for k, (a, b) in enumerate(((xhi, wr_hi), (xhi, wr_lo), (xlo, wr_hi))):
                        i = pe.matmul(bank[7][:, m * 8:(m + 1) * 8], a[:, t], b[:], start=k == 0, stop=k == 2)
                i.then_inc(lg_ps, 1)

            def weight_transposes():
                pe.wait_ge(var_w, 1)
                for m in range(NT):
                    i = pe.transpose(bank[4][0:16, m * P:(m + 1) * P], W16[:, m], ident[:])
                i.then_inc(wT_ps, 1)

            def spread_weight(e):
                if e == 0:
                    pe.wait_ge(wT_ok, 1)
                else:
                    pe.wait_ge(yw_ok, e)
                pe.matmul(bank[4][:], pick16[:, e], WT[:], start=True, stop=True).then_inc(wB_ps, 1)

            def gate_up(n):
                e, c = n // 3, n % 3
                c0, w = CH[c]
                if n >= 2:
                    pe.wait_ge(h_ok, n - 1)
                for part, (bk_, sem_) in enumerate(((n % 2, g_ps), (2 + n % 2, u_ps))):
                    o = (e * 2 + part) * I + c0
                    for k, (wt, xx) in enumerate(((gu_hi, xhi), (gu_hi, xlo), (gu_lo, xhi))):
                        i = pe.matmul(bank[bk_][0:w, :], wt[:, o:o + w], xx[:], start=k == 0, stop=k == 2)
                    i.then_inc(sem_, 1)

            def down(e):
                pe.wait_ge(lo_ok, 3 * e + 3)
                pe.wait_ge(wB_ok, e + 1)
                for c in range(3):
                    w = CH[c][1]
                    sl = (3 * e + c) % HS
                    for k, (wt, hh) in enumerate(((wd_hi, h_hi), (wd_hi, h_lo), (wd_lo, h_hi))):
                        i = pe.matmul(bank[4][:], wt[0:w, c, e * D:(e + 1) * D], hh[0:w, sl],
                                      start=c == 0 and k == 0, stop=c == 2 and k == 2)
                i.then_inc(y_ps, 1)

            def sum_transposes(k):
                if k > 1:
                    pe.wait_ge(acc_ok, E)
                for m in range(NT):
                    i = pe.transpose(bank[4][:, m * P:(m + 1) * P], acc[:, m * P:(m + 1) * P], ident[:])
                i.then_inc(fT_ps, 1)

            def attend(n):
                if n == 1:
                    pe.wait_ge(xn_ok, 1)
                    for m in range(NT):
                        i = pe.transpose(bank[5][:, m * P:(m + 1) * P], xn[:, m], ident[:])
                    i.then_inc(xnT_ps, 1)
                    pe.matmul(bank[7][:], wk_sb[:], ctx[:, :, 0], start=True, stop=True).then_inc(k_ps, 1)
                if n == 2:
                    pe.wait_ge(xnT_ok, 1)
                    pe.matmul(bank[6][:], wq_sb[:], xnT[:], start=True, stop=True).then_inc(q_ps, 1)
                if n == 3:
                    pe.wait_ge(qsq_ok, 1)
                    for b in range(GB):
                        i = pe.matmul(bank[5][:, 0:L], headsum[:, b], qsq[:, b * L:(b + 1) * L],
                                      start=b == 0, stop=b == GB - 1)
                    i.then_inc(norm_ps, 1)
                    values(0)
                if n == 5:
                    pe.wait_ge(seld_ok, 1)
                    pe.transpose(bank[6][:, 0:P], seld[:].rearrange("p a l -> p (a l)"),
                                 ident[:]).then_inc(selT_ps, 1)
                    values(1)
                if n in SCORES_AT:
                    scores(SCORES_AT[n])
                if n in TRANSPOSE_AT:
                    prob_transposes(TRANSPOSE_AT[n])
                if n in CONTEXT_AT:
                    context(2 * CONTEXT_AT[n])
                    context(2 * CONTEXT_AT[n] + 1)
                if n in NORMALISE_AT:
                    ctx_transpose(NORMALISE_AT[n])
                if n in PROJECT_AT:
                    project(PROJECT_AT[n])

            def iteration(experts, attention, finishing):
                for n in range(NS):
                    if experts:
                        gate_up(n)
                        if n == 0 and finishing:
                            sum_transposes(1)
                        if n == 2:
                            if finishing:
                                pe.wait_ge(fin_ok, 1)
                            weight_transposes()
                        if n % 3 == 0 and n >= 3:
                            spread_weight(n // 3 - 1)
                        if n % 3 == 1 and n >= 4:
                            down((n - 4) // 3)
                    if attention:
                        if experts and n == 1:
                            pe.wait_ge(lg_ok, 1)
                        attend(n)
                if attention:
                    second_transposes()
                if experts:
                    spread_weight(E - 1)
                    down(E - 1)
                if attention:
                    logits()

            pe.wait_ge(c_ident, 1)
            pe.wait_ge(c_masks, 1)
            pe.wait_ge(c_zero, 11)
            pe.wait_ge(wqkv_in, 64)
            pe.wait_ge(ctx_in, 32)
            pe.wait_ge(wr_ok, 2)
            iteration(False, True, False)
            meet(pe)
            pe.wait_ge(pick_ok, 1)
            pe.wait_ge(wgt_lo, 2)
            pe.wait_ge(wgt_c_lo, 3)
            iteration(True, True, False)
            meet(pe)
            with pe.Fori(2, NG):
                iteration(True, True, True)
                meet(pe)
            iteration(True, False, True)
            pe.wait_ge(yw_ok, E)
            sum_transposes(2)


def kernel(**inputs):
    import numpy as np
    import concourse.bacc as bacc
    from concourse import mybir as _mybir
    from concourse.bass_utils import run_bass_kernel_spmd as run

    a = {k: np.asarray(v) for k, v in inputs.items()}
    heads = np.arange(D).reshape(4, 2, 2, DK).transpose(0, 2, 1, 3).reshape(-1)
    gate = np.concatenate([a["L0_ffn_sg"][None], a["L0_ffn_rg"]])
    up = np.concatenate([a["L0_ffn_su"][None], a["L0_ffn_ru"]])
    down = np.concatenate([a["L0_ffn_sd"][None], a["L0_ffn_rd"]])
    arrays = {
        "x": a["x"].reshape(B * L, D),
        "ctxT": a["ctx_1024"].reshape(B * L, D).T,
        "gates": np.concatenate([a["g_xattn"], a["g_ffn"]]),
        "wq": a["L0_xattn_Wq"], "bq": a["L0_xattn_bq"], "wk": a["L0_xattn_Wk"], "bk": a["L0_xattn_bk"],
        "wv": a["L0_xattn_Wv"], "bv": a["L0_xattn_bv"], "wo": a["L0_xattn_Wo"][heads], "bo": a["L0_xattn_bo"],
        "wgu": np.stack([gate, up], 1).transpose(3, 0, 1, 2).reshape(D, -1),
        "wd": down.transpose(0, 2, 1),
        "wrT": a["L0_ffn_wr"].T, "rb": a["L0_ffn_rb"],
    }
    arrays = {k: np.ascontiguousarray(v) for k, v in arrays.items()}
    nc = bacc.Bacc("TRN2", target_bir_lowering=False, num_devices=1)
    args = [nc.dram_tensor(f"in_{k}", v.shape, _mybir.dt.from_np(v.dtype), kind="ExternalInput").ap()
            for k, v in arrays.items()]
    y = nc.dram_tensor("out_y", (B * L, D), _mybir.dt.float32, kind="ExternalOutput").ap()
    gated_block(nc, *args, y)
    r = run(nc, [{f"in_{k}": v for k, v in arrays.items()}], core_ids=[0])
    return r.results[0]["out_y"].reshape(B, L, D)
```

```python
from contextlib import ExitStack

import concourse.bass as bass
from concourse import mybir

F32 = mybir.dt.float32
F32R = mybir.dt.float32r
BF16 = mybir.dt.bfloat16
ALU = mybir.AluOpType
ACT = mybir.ActivationFunctionType
AX = mybir.AxisListType

P = 128
D = 128
B, L = 64, 64
H, DK = 16, 8
U = L // 2
I = 352
E = 8
GB = 8
NG = B // GB
GT = GB * L
NT = GT // P
CH = [(0, 128), (128, 128), (256, 96)]
NC_ = len(CH)
NS = E * NC_
HS = 7
VW = DK + 1
SCORES_AT = {8 + 3 * (b // 2) + b % 2: b for b in range(GB)}
TRANSPOSE_AT = {n + 1: b for n, b in SCORES_AT.items()}
CONTEXT_AT = {11 + 3 * m: m for m in range(NT)}
NORMALISE_AT = {n + 1: m for n, m in CONTEXT_AT.items()}
PROJECT_AT = {n + 2: m for n, m in CONTEXT_AT.items()}
QEXP_AT = {n - 3: b for n, b in SCORES_AT.items()}
DOWN_AT = {7: 0, 9: 1, 11: 2, **{3 * e + 4: e for e in range(3, E - 1)}}
SPREAD_AT = {n - 1: e for n, e in DOWN_AT.items()}
WEIGH_AT = {n + 1: e for n, e in DOWN_AT.items()}
WT_AT = 6
GUP = 4
SPLIT_AT = {8 + 2 * k: k for k in range(GUP + NC_)}
BIG = 1e30
EPS = 1e-5
SCALE = float(DK) ** -0.5


def gated_block(nc, x, ctxT, gates, wq, bq, wk, bk, wv, bv, wo, bo, wgu, wd, wrT, rb, out):
    st = ExitStack()
    with st:
        def sb(name, shape, dt=F32):
            return st.enter_context(nc.sbuf_tensor(name, shape, dt))

        def sem(name):
            return st.enter_context(nc.semaphore(name))

        bank = [st.enter_context(nc.psum_tensor(f"bank{i}", [P, 512], F32)) for i in range(8)]

        ident = sb("ident", [P, P])
        quadpick = sb("quadpick", [P, GB, 4, L], BF16)
        picked = sb("picked", [P, GB, 4])
        quadmask = sb("quadmask", [P, 4])
        headsum = sb("headsum", [P, GB, P])
        rowmask = sb("rowmask", [P, 4])
        halfmask = sb("halfmask", [P, 2])
        pick16 = sb("pick16", [16, E, P], F32R)
        firstof = sb("firstof", [P, E - 1])
        negh = sb("negh", [P, NT])
        wq_sb, wk_sb, wv_sb, wo_sb = (sb(n, [P, D]) for n in ("wq_sb", "wk_sb", "wv_sb", "wo_sb"))
        bqk = sb("bqk", [P, 2])
        bv_b = sb("bv_b", [P, D])
        bo_b = sb("bo_b", [P, D])
        tbo = sb("tbo", [P, D])
        rb_b = sb("rb_b", [P, E - 1])
        gate_in = sb("gate_in", [P, 2])
        tgate = sb("tgate", [P, 2])
        wr_sb = sb("wr_sb", [P, 8])
        wr_hi = sb("wr_hi", [P, 8], F32R)
        wr_lo = sb("wr_lo", [P, 8], F32R)
        GUW = E * 2 * I
        gu_hi = sb("gu_hi", [P, GUW], F32R)
        gu_lo = sb("gu_lo", [P, GUW], F32R)
        wd_hi = sb("wd_hi", [P, NC_, E * D], F32R)
        wd_lo = sb("wd_lo", [P, NC_, E * D], F32R)

        xg = sb("xg", [P, NT, D])
        xpb = sb("xpb", [P, NT, D])
        x2 = sb("x2", [P, NT, D])
        ctx = sb("ctx", [P, GB, 2, L])
        stats = sb("stats", [P, NT, 6])
        mv = sb("mv", [P, NT, 2])
        ve = sb("ve", [P, NT])
        rstd = sb("rstd", [P, NT])
        stats2 = sb("stats2", [P, NT, 6])
        mv2 = sb("mv2", [P, NT, 2])
        ve2 = sb("ve2", [P, NT])
        rstd2 = sb("rstd2", [P, NT])
        xn = sb("xn", [P, NT, D])
        xnT = sb("xnT", [P, GT])
        q = sb("q", [P, GT])
        qsq = xnT
        qexp = sb("qexp", [P, GB, 4, L])
        kquad = sb("kquad", [P, 4, GT])
        top8 = sb("top8", [P, 4, 8])
        rest = sb("rest", [P, 4, L])
        keybias = sb("keybias", [P, 4, L], BF16)
        bias = sb("bias", [P, L])
        seld = sb("seld", [P, 2, L])
        selP = sb("selP", [P, NT, H])
        vblk = sb("vblk", [P, GB * 8, 2, VW])
        mx = sb("mx", [P, 2, 8])
        prob = sb("prob", [P, 2, 8, L])
        pick16f = prob[0:16].rearrange("p s a k -> p (s a k)").rearrange("p (e n) -> p e n", e=E)
        probT = sb("probT", [P, 2, 512])
        vtmp = probT[:, 0].rearrange("p (b d) -> p b d", b=4)
        rec = sb("rec", [P, 2, H])
        recs = sb("recs", [P, 2, H])
        cn = sb("cn", [P, 2, D])
        cnT = sb("cnT", [P, 2, D])
        xn2 = xn
        xhi = sb("xhi", [P, GT], F32R)
        xlo = sb("xlo", [P, GT], F32R)
        lg = sb("lg", [P, NT, 7])
        lt = sb("lt", [P, NT, 7])
        oh1 = sb("oh1", [P, NT, 7])
        oh2 = sb("oh2", [P, NT, 7])
        rs = sb("rs", [P, 8, NT])
        W = sb("W", [P, NT, 8])
        W16 = sb("W16", [P, NT, 16])
        whi = sb("whi", [P, NT, 8], F32R)
        WT = sb("WT", [16, GT], F32R)
        work = sb("work", [P, 6144])
        wB = work[:, 0:1024].rearrange("p (s t) -> p s t", s=2)
        acc = work[:, 1024:1536]
        yw = work[:, 1536:2048]
        fin = work[:, 2048:2560].rearrange("p (m d) -> p m d", m=NT)
        x2keep = work[:, 2560:3072].rearrange("p (m d) -> p m d", m=NT)
        tg = work[:, 3072:4096].rearrange("p (s t) -> p s t", s=2)
        ag = work[:, 4096:5120].rearrange("p (s t) -> p s t", s=2)
        hg = work[:, 5120:6144].rearrange("p (s t) -> p s t", s=2)
        h_hi = sb("h_hi", [P, HS, GT], F32R)
        h_lo = sb("h_lo", [P, HS, GT], F32R)

        small_in = sem("small_in")
        wqkv_in = sem("wqkv_in")
        c_ident = sem("c_ident")
        c_gp = sem("c_gp")
        c_masks = sem("c_masks")
        c_zero = sem("c_zero")
        c_pick = sem("c_pick")
        rowmask_ok = sem("rowmask_ok")
        pick_ok = sem("pick_ok")
        tgate_ok = sem("tgate_ok")
        tbo_ok = sem("tbo_ok")
        wr_ok = sem("wr_ok")
        gu_in = [sem(f"gu_in{k}") for k in range(GUP)]
        wd_in = [sem(f"wd_in{c}") for c in range(NC_)]
        wgt_hi = sem("wgt_hi")
        wgt_lo = sem("wgt_lo")
        x_in = sem("x_in")
        ctx_in = sem("ctx_in")
        out_done = sem("out_done")
        bn_ok = sem("bn_ok")
        mv_ok = sem("mv_ok")
        var_ok = sem("var_ok")
        rstd_ok = sem("rstd_ok")
        xn_ok = sem("xn_ok")
        xpb_ok = sem("xpb_ok")
        xnT_ps = sem("xnT_ps")
        xnT_ok = sem("xnT_ok")
        q_ps = sem("q_ps")
        k_ps = sem("k_ps")
        q_ok = sem("q_ok")
        k_ok = sem("k_ok")
        qsq_ok = sem("qsq_ok")
        qexp_ok = sem("qexp_ok")
        norm_ps = sem("norm_ps")
        top_ok = sem("top_ok")
        bias_ok = sem("bias_ok")
        mask_ok = sem("mask_ok")
        seld_ok = sem("seld_ok")
        selT_ps = sem("selT_ps")
        selP_ok = sem("selP_ok")
        v_ps = sem("v_ps")
        vtmp_ok = sem("vtmp_ok")
        vblk_ok = sem("vblk_ok")
        s_ps = sem("s_ps")
        mx_ok = sem("mx_ok")
        sub_ok = sem("sub_ok")
        exp_ok = sem("exp_ok")
        pT_ps = sem("pT_ps")
        pT_ok = sem("pT_ok")
        pv_ps = sem("pv_ps")
        rec_ok = sem("rec_ok")
        recs_ok = sem("recs_ok")
        cn_ok = sem("cn_ok")
        cT_ps = sem("cT_ps")
        cT_ok = sem("cT_ok")
        o_ps = sem("o_ps")
        x2_ok = sem("x2_ok")
        bn2_ok = sem("bn2_ok")
        mv2_ok = sem("mv2_ok")
        var2_ok = sem("var2_ok")
        rstd2_ok = sem("rstd2_ok")
        xn2_ok = sem("xn2_ok")
        xn2T_ps = sem("xn2T_ps")
        xhi_ok = sem("xhi_ok")
        xlo_ok = sem("xlo_ok")
        lg_ps = sem("lg_ps")
        lg_ok = sem("lg_ok")
        rt_ok = sem("rt_ok")
        dif_ok = sem("dif_ok")
        edif_ok = sem("edif_ok")
        w_ok = sem("w_ok")
        var_w = sem("var_w")
        wT_ps = sem("wT_ps")
        wT_ok = sem("wT_ok")
        wB_ps = sem("wB_ps")
        wB_ok = sem("wB_ok")
        g_ps = sem("g_ps")
        u_ps = sem("u_ps")
        t_ok = sem("t_ok")
        a_ok = sem("a_ok")
        h_ok = sem("h_ok")
        hi_ok = sem("hi_ok")
        lo_ok = sem("lo_ok")
        y_ps = sem("y_ps")
        yw_ok = sem("yw_ok")
        acc_ok = sem("acc_ok")
        fT_ps = sem("fT_ps")
        keep_ok = sem("keep_ok")
        fin_ok = sem("fin_ok")

        arrived = sem("arrived")
        go = {e.engine: sem(f"go_{n}") for n, e in (("sync", nc.sync), ("scalar", nc.scalar), ("vector", nc.vector),
                                                     ("tensor", nc.tensor))}

        block = st.enter_context(nc.Block())
        counted = range(x_in.num, fin_ok.num + 1)

        def meet(eng):
            eng.drain().then_inc(arrived, 1)
            eng.wait_ge(go[eng.engine], 1)
            eng.sem_inc(go[eng.engine], -1)

        def meet_pool(gp):
            gp.drain()
            gp.wait_ge(arrived, 4)
            gp.sem_inc(arrived, -4)
            gp.sem_clear(counted)
            for sem_ in go.values():
                gp.sem_inc(sem_, 1)

        def raw_weights(k):
            w = GUW // GUP
            if k < GUP:
                return work[:, k * w:(k + 1) * w]
            c = k - GUP
            return work[0:CH[c][1], c * w:c * w + E * D]

        def split_weights(k, gate_up, down):
            if k < GUP:
                return gate_up[:, k * GUW // GUP:(k + 1) * GUW // GUP]
            return down[0:CH[k - GUP][1], k - GUP]

        x_v = x.rearrange("(t p) d -> p t d", p=P)
        out_v = out.rearrange("(t p) d -> p t d", p=P)

        @block.sync
        def _(sp):
            def load_x(g):
                sp.dma_start(xg[:], x_v[:, bass.ds(g * NT, NT), :]).then_inc(x_in, 16)

            def load_ctx(g):
                src = ctxT[:, bass.ds(g * GT, GT)].rearrange("p (b l) -> p b l", b=GB)
                for twice in range(2):
                    sp.dma_start(ctx[:, :, twice], src).then_inc(ctx_in, 16)

            def next_group(g):
                sp.wait_ge(xn_ok, 1)
                sp.wait_ge(xpb_ok, 1)
                load_x(g)
                sp.wait_ge(k_ps, 1)
                sp.wait_ge(v_ps, 2)
                load_ctx(g)

            def store(g):
                sp.wait_ge(fin_ok, 1)
                sp.dma_start(out_v[:, bass.ds(g * NT, NT), :], fin).then_inc(out_done, 16)

            def landed():
                sp.wait_ge(x_in, 16)
                sp.wait_ge(ctx_in, 32)

            load_x(0)
            for dst, src in ((wq_sb, wq), (wk_sb, wk), (wv_sb, wv), (wo_sb, wo)):
                sp.dma_start(dst[:], src).then_inc(wqkv_in, 16)
            load_ctx(0)
            for dst, src in ((bqk[:, 0:1], bq.unsqueeze(1)), (bqk[:, 1:2], bk.unsqueeze(1)),
                             (wr_sb[:, 0:7], wrT),
                             (bv_b[:], bv.unsqueeze(0).broadcast_to([P, D])),
                             (bo_b[:], bo.unsqueeze(0).broadcast_to([P, D])),
                             (rb_b[:], rb.unsqueeze(0).broadcast_to([P, 7])),
                             (gate_in[:], gates.unsqueeze(0).broadcast_to([P, 2]))):
                sp.dma_start(dst, src).then_inc(small_in, 16)
            for k in range(GUP):
                sp.dma_start(raw_weights(k), wgu[:, k * GUW // GUP:(k + 1) * GUW // GUP]).then_inc(gu_in[k], 16)
            next_group(1)
            for c, (c0, w) in enumerate(CH):
                sp.wait_ge(wgt_lo, c + 1)
                sp.dma_start(raw_weights(GUP + c).rearrange("p (e h) -> p e h", e=E),
                             wd[:, c0:c0 + w, :].rearrange("e i h -> i e h")).then_inc(wd_in[c], 16)
            sp.wait_ge(x_in, 32)
            sp.wait_ge(ctx_in, 64)
            meet(sp)
            next_group(2)
            landed()
            meet(sp)
            with sp.Fori(2, NG - 1) as g:
                store(g - 2)
                next_group(g + 1)
                landed()
                sp.wait_ge(out_done, 16)
                meet(sp)
            store(NG - 3)
            sp.wait_ge(out_done, 16)
            meet(sp)
            store(NG - 2)
            sp.wait_ge(fin_ok, 2)
            sp.dma_start(out_v[:, (NG - 1) * NT:NG * NT, :], fin).then_inc(out_done, 16)
            sp.wait_ge(out_done, 32)

        @block.gpsimd
        def _(gp):
            gp.memset(ident[:], 0.0).then_inc(c_gp, 1)
            gp.memset(headsum[:], 1.0).then_inc(c_gp, 1)
            gp.memset(pick16f, 0.0).then_inc(c_gp, 1)
            gp.memset(wr_sb[:, 7:8], 0.0).then_inc(c_gp, 1)
            gp.memset(negh[:], -0.5).then_inc(c_gp, 1)
            for e in range(E - 1):
                gp.memset(firstof[:, e:e + 1], float(7 - e)).then_inc(c_gp, 1)
            gp.wait_ge(c_gp, 12)
            gp.affine_select(out=ident[:], in_=ident[:], compare_op=ALU.not_equal, fill=1.0, base=0,
                             pattern=[[-1, P]], channel_multiplier=1).then_inc(c_ident, 1)
            gp.affine_select(out=headsum[:], in_=headsum[:], compare_op=ALU.is_ge, fill=0.0, base=0,
                             pattern=[[P, GB], [-DK, P]], channel_multiplier=1).then_inc(c_gp, 1)
            gp.affine_select(out=pick16f, in_=pick16f, compare_op=ALU.not_equal, fill=1.0, base=0,
                             pattern=[[-1, E], [0, P]], channel_multiplier=1).then_inc(c_gp, 1)
            gp.wait_ge(c_gp, 14)
            gp.affine_select(out=headsum[:], in_=headsum[:], compare_op=ALU.is_ge, fill=0.0, base=DK - 1,
                             pattern=[[-P, GB], [DK, P]], channel_multiplier=-1).then_inc(c_masks, 1)
            gp.affine_select(out=pick16f, in_=pick16f, compare_op=ALU.not_equal, fill=1.0, base=-E,
                             pattern=[[-1, E], [0, P]], channel_multiplier=1).then_inc(c_pick, 1)

            def expand_queries(b):
                gp.tensor_tensor(
                    qexp[:, b], q[:, b * L:(b + 1) * L].unsqueeze(1).broadcast_to([P, 4, L]),
                    rowmask[:].unsqueeze(2).broadcast_to([P, 4, L]), ALU.mult).then_inc(qexp_ok, 1)

            def attend(n):
                if n == 0:
                    gp.wait_ge(var_ok, 1)
                    gp.tensor_tensor(rstd[:], ve[:], negh[:], ALU.pow).then_inc(rstd_ok, 1)
                if n == 1:
                    gp.wait_ge(tbo_ok, 1)
                    gp.tensor_tensor(xpb[:], xg[:], tbo[:].unsqueeze(1).broadcast_to([P, NT, D]),
                                     ALU.add).then_inc(xpb_ok, 1)
                if n == 2:
                    gp.wait_ge(q_ok, 1)
                    gp.wait_ge(rowmask_ok, 1)
                if n in QEXP_AT:
                    expand_queries(QEXP_AT[n])
                if n == 22:
                    gp.wait_ge(var2_ok, 1)
                    gp.tensor_tensor(rstd2[:], ve2[:], negh[:], ALU.pow).then_inc(rstd2_ok, 1)

            def weights_lo(k):
                gp.wait_ge(wgt_hi, k + 1)
                gp.tensor_tensor(split_weights(k, gu_lo, wd_lo), raw_weights(k),
                                 split_weights(k, gu_hi, wd_hi).bitcast(F32), ALU.subtract).then_inc(wgt_lo, 1)

            def lo_part(n):
                w = CH[n % 3][1]
                gp.wait_ge(hi_ok, n + 1)
                gp.tensor_tensor(h_lo[0:w, n % HS], hg[0:w, n % 2], h_hi[0:w, n % HS].bitcast(F32),
                                 ALU.subtract).then_inc(lo_ok, 1)

            def add_expert(e):
                gp.wait_ge(yw_ok, e + 1)
                if e == 0:
                    gp.tensor_copy(acc, yw).then_inc(acc_ok, 1)
                else:
                    gp.wait_ge(acc_ok, e)
                    gp.tensor_tensor(acc, acc, yw, ALU.add).then_inc(acc_ok, 1)

            def iteration(experts, attention):
                for n in range(NS):
                    if attention and n == 0:
                        attend(0)
                    if experts and n >= 1:
                        lo_part(n - 1)
                    if experts and n in WEIGH_AT:
                        add_expert(WEIGH_AT[n])
                    if attention and n > 0:
                        attend(n)
                    if not experts and n in SPLIT_AT:
                        weights_lo(SPLIT_AT[n])
                if experts:
                    lo_part(NS - 1)
                    add_expert(E - 1)

            iteration(False, True)
            meet_pool(gp)
            iteration(True, True)
            meet_pool(gp)
            with gp.Fori(2, NG):
                iteration(True, True)
                meet_pool(gp)
            iteration(True, False)

        @block.scalar
        def _(act):
            act.wait_ge(small_in, 16 * 7)
            act.activation(tgate[:], gate_in[:], ACT.Tanh).then_inc(tgate_ok, 1)

            def weights_hi(k):
                act.wait_ge(gu_in[k] if k < GUP else wd_in[k - GUP], 16)
                act.copy(split_weights(k, gu_hi, wd_hi), raw_weights(k)).then_inc(wgt_hi, 1)

            def spread_values(hv):
                act.wait_ge(vtmp_ok, hv + 1)
                for px in range(2):
                    src = vtmp.rearrange("p b (j x c d) -> p (b j) x c d", j=4, x=2, c=2)[:, :, px]
                    dst = vblk[:, hv * 32:hv * 32 + 32, px, 0:DK].rearrange("p (n c) d -> p n c d", c=2)
                    act.activation(dst, src, ACT.Copy, scale=halfmask[:, px:px + 1]).then_inc(vblk_ok, 1)

            def probT_copy(b):
                act.wait_ge(pT_ps, b + 1)
                if b == 0:
                    act.wait_ge(vblk_ok, 4)
                if b >= 2:
                    act.wait_ge(pv_ps, b - 1)
                act.copy(probT[:, b % 2], bank[6][:]).then_inc(pT_ok, 1)

            def ctx_copy(m):
                act.wait_ge(cT_ps, m + 1)
                if m >= 2:
                    act.wait_ge(o_ps, m - 1)
                act.copy(cnT[:, m % 2], bank[7][:, 0:D]).then_inc(cT_ok, 1)

            def round_h(n):
                w = CH[n % 3][1]
                act.wait_ge(h_ok, n + 1)
                if n >= HS:
                    act.wait_ge(y_ps, (n - HS) // 3 + 1)
                act.copy(h_hi[0:w, n % HS], hg[0:w, n % 2]).then_inc(hi_ok, 1)

            def gate_tanh(n):
                w = CH[n % 3][1]
                act.wait_ge(g_ps, n + 1)
                if n >= 2:
                    act.wait_ge(a_ok, n - 1)
                act.activation(tg[0:w, n % 2], bank[n % 2][0:w, :], ACT.Tanh, scale=0.5).then_inc(t_ok, 1)

            def weight_copy(e):
                act.wait_ge(wB_ps, e + 1)
                act.copy(wB[:, e % 2], bank[4][:]).then_inc(wB_ok, 1)

            def attend(n):
                if n == 1:
                    act.wait_ge(xnT_ps, 1)
                    act.copy(xnT[:], bank[5][:]).then_inc(xnT_ok, 1)
                if n == 2:
                    act.wait_ge(q_ps, 1)
                    act.activation(q[:], bank[6][:], ACT.Identity, bias=bqk[:, 0:1]).then_inc(q_ok, 1)
                    act.activation(qsq[:], bank[6][:], ACT.Square, bias=bqk[:, 0:1]).then_inc(qsq_ok, 1)
                    act.wait_ge(c_zero, 1)
                    for j in range(4):
                        r = slice(32 * j, 32 * j + 32)
                        act.activation(kquad[r, j], bank[7][r, :], ACT.Identity,
                                       bias=bqk[r, 1:2]).then_inc(k_ok, 1)
                if n == 5:
                    spread_values(0)
                if n == 7:
                    spread_values(1)

            def exponentials(b):
                act.wait_ge(sub_ok, b + 1)
                act.activation(prob[:, b % 2], prob[:, b % 2], ACT.Exp, scale=SCALE).then_inc(exp_ok, 1)

            def iteration(experts, attention):
                for n in range(NS):
                    if attention and n - 1 in TRANSPOSE_AT:
                        probT_copy(TRANSPOSE_AT[n - 1])
                    if attention and n in PROJECT_AT:
                        ctx_copy(PROJECT_AT[n])
                    if experts:
                        gate_tanh(n)
                    if attention and n in TRANSPOSE_AT:
                        exponentials(TRANSPOSE_AT[n])
                    if experts:
                        if n >= 1:
                            round_h(n - 1)
                        if n == WT_AT:
                            act.wait_ge(wT_ps, 1)
                            act.copy(WT[:], bank[4][0:16, :]).then_inc(wT_ok, 1)
                        if n == 4:
                            act.wait_ge(dif_ok, 1)
                            act.activation(rs[:, 3], rs[:, 2], ACT.Exp).then_inc(edif_ok, 1)
                        if n in SPREAD_AT:
                            weight_copy(SPREAD_AT[n])
                    if attention:
                        attend(n)
                    if not experts and n in SPLIT_AT:
                        weights_hi(SPLIT_AT[n])
                if experts:
                    round_h(NS - 1)
                    weight_copy(E - 1)
                if attention:
                    act.wait_ge(xn2T_ps, 1)
                    if experts:
                        act.wait_ge(u_ps, NS)
                    act.copy(xhi[:], bank[6][:]).then_inc(xhi_ok, 1)

            iteration(False, True)
            meet(act)
            iteration(True, True)
            meet(act)
            with act.Fori(2, NG):
                iteration(True, True)
                meet(act)
            iteration(True, False)

        @block.vector
        def _(dve):
            dve.memset(kquad[:], 0.0).then_inc(c_zero, 1)
            dve.memset(vblk[:], 0.0).then_inc(c_zero, 1)
            dve.memset(W[:], 0.5).then_inc(c_zero, 1)
            dve.memset(halfmask[:], 0.0).then_inc(c_zero, 1)
            dve.wait_ge(c_zero, 4)
            dve.memset(halfmask[0:64, 0:1], 1.0).then_inc(c_zero, 1)
            dve.memset(halfmask[64:128, 1:2], 1.0).then_inc(c_zero, 1)
            dve.memset(vblk[0:64, :, 0, DK:VW], 1.0).then_inc(c_zero, 1)
            dve.memset(vblk[64:128, :, 1, DK:VW], 1.0).then_inc(c_zero, 1)
            def masks():
                dve.wait_ge(c_ident, 1)
                dve.tensor_reduce(picked[:], ident[:].rearrange("p (b j r) -> p b r j", b=GB, j=4), AX.X,
                                  ALU.add).then_inc(c_zero, 1)
                dve.tensor_reduce(quadmask[:], ident[:].rearrange("p (b j r) -> p j b r", b=GB, j=4), AX.XY,
                                  ALU.add).then_inc(c_zero, 1)
                dve.wait_ge(c_zero, 10)
                dve.tensor_copy(quadpick[:], picked[:].unsqueeze(3).broadcast_to([P, GB, 4, L])).then_inc(c_zero, 1)
                dve.wait_ge(c_masks, 1)
                dve.tensor_reduce(rowmask[:], headsum[:, 0, 0:H].rearrange("p (j r) -> p r j", r=4), AX.X,
                                  ALU.add).then_inc(rowmask_ok, 1)
                dve.wait_ge(c_pick, 1)
                dve.tensor_copy(pick16[:], pick16f).then_inc(pick_ok, 1)

            def first_stats():
                for m in range(NT):
                    i = dve.bn_stats(stats[:, m], xg[:, m])
                i.then_inc(bn_ok, 1)
                dve.wait_ge(bn_ok, 1)
                for m in range(NT):
                    i = dve.bn_aggr(mv[:, m], stats[:, m])
                i.then_inc(mv_ok, 1)
                dve.wait_ge(mv_ok, 1)
                dve.tensor_scalar(ve[:], mv[:, :, 1], EPS, None, ALU.add).then_inc(var_ok, 1)

            def first_norm():
                dve.wait_ge(rstd_ok, 1)
                for m in range(NT):
                    i = dve.tensor_scalar(xn[:, m], xg[:, m], mv[:, m, 0:1], rstd[:, m:m + 1],
                                          ALU.subtract, ALU.mult)
                i.then_inc(xn_ok, 1)

            def once():
                dve.wait_ge(small_in, 16 * 7)
                dve.wait_ge(tgate_ok, 1)
                dve.tensor_scalar(tbo[:], bo_b[:], tgate[:, 0:1], None, ALU.mult).then_inc(tbo_ok, 1)
                dve.wait_ge(c_gp, 4)
                dve.tensor_copy(wr_hi[:], wr_sb[:]).then_inc(wr_ok, 1)
                dve.wait_ge(wr_ok, 1)
                dve.tensor_tensor(wr_lo[:], wr_sb[:], wr_hi[:].bitcast(F32), ALU.subtract).then_inc(wr_ok, 1)

            def choose():
                dve.wait_ge(norm_ps, 1)
                src = bank[5][:, 0:L]
                for r in range(4):
                    dve.max(top8[:, r], src).then_inc(top_ok, 1)
                    dve.wait_ge(top_ok, 2 * r + 1)
                    dve.match_replace(rest[:, r], top8[:, r], src, -1.0).then_inc(top_ok, 1)
                    dve.wait_ge(top_ok, 2 * r + 2)
                    src = rest[:, r]
                dve.tensor_scalar(bias[:], src, 0.0, -BIG, ALU.is_ge, ALU.mult).then_inc(bias_ok, 1)
                dve.tensor_scalar(seld[:], src.unsqueeze(1).broadcast_to([P, 2, L]), 0.0, None,
                                  ALU.is_lt).then_inc(seld_ok, 1)
                dve.wait_ge(bias_ok, 1)
                dve.tensor_tensor(keybias[:], bias[:].unsqueeze(1).broadcast_to([P, 4, L]),
                                  quadmask[:].unsqueeze(2).broadcast_to([P, 4, L]), ALU.mult).then_inc(mask_ok, 1)

            def value_bias(hv):
                dve.wait_ge(v_ps, hv + 1)
                if hv:
                    dve.wait_ge(vblk_ok, 2)
                dve.tensor_tensor(vtmp, bank[7][:].rearrange("p (b d) -> p b d", b=4),
                                  bv_b[:].unsqueeze(1).broadcast_to([P, 4, D]), ALU.add).then_inc(vtmp_ok, 1)

            def query_mask():
                dve.wait_ge(selT_ps, 1)
                sT = bank[6][:, 0:P].rearrange("p (m x h) -> p m x h", m=NT, x=2)
                dve.tensor_copy(selP[0:64], sT[0:64, :, 0]).then_inc(selP_ok, 1)
                dve.tensor_copy(selP[64:128], sT[64:128, :, 1]).then_inc(selP_ok, 1)

            def normalise(m):
                dve.wait_ge(pv_ps, 2 * m + 2)
                c = bank[7][:, 0:H * VW].rearrange("p (n v) -> p n v", v=VW)
                dve.reciprocal(rec[:, m % 2], c[:, :, DK]).then_inc(rec_ok, 1)
                dve.wait_ge(rec_ok, m + 1)
                dve.wait_ge(selP_ok, 2)
                dve.tensor_tensor(recs[:, m % 2].rearrange("p (j c x) -> p j c x", j=4, c=2),
                                  rec[:, m % 2].rearrange("p (j c x) -> p j c x", j=4, c=2),
                                  selP[:, m].rearrange("p (j x c) -> p j c x", j=4, x=2),
                                  ALU.mult).then_inc(recs_ok, 1)
                dve.wait_ge(recs_ok, m + 1)
                if m >= 2:
                    dve.wait_ge(cT_ps, m - 1)
                dve.tensor_tensor(cn[:, m % 2].rearrange("p (n d) -> p n d", d=DK), c[:, :, 0:DK],
                                  recs[:, m % 2].unsqueeze(2).broadcast_to([P, H, DK]),
                                  ALU.mult).then_inc(cn_ok, 1)

            def residual(m):
                dve.wait_ge(o_ps, m + 1)
                dve.wait_ge(xpb_ok, 1)
                dve.scalar_tensor_tensor(x2[:, m], bank[7][:, 0:D], tgate[:, 0:1], xpb[:, m],
                                         ALU.mult, ALU.add).then_inc(x2_ok, 1)
                dve.wait_ge(x2_ok, m + 1)
                dve.bn_stats(stats2[:, m], x2[:, m]).then_inc(bn2_ok, 1)
                dve.wait_ge(bn2_ok, m + 1)
                dve.bn_aggr(mv2[:, m], stats2[:, m]).then_inc(mv2_ok, 1)

            def softmax_shift(b):
                sc = bank[5][:].rearrange("p (n k) -> p n k", n=8)
                dve.wait_ge(s_ps, b + 1)
                dve.tensor_reduce(mx[:, b % 2], sc, AX.X, ALU.max).then_inc(mx_ok, 1)
                dve.wait_ge(mx_ok, b + 1)
                if b >= 2:
                    dve.wait_ge(pT_ps, b - 1)
                dve.tensor_tensor(prob[:, b % 2], sc, mx[:, b % 2].unsqueeze(2).broadcast_to([P, 8, L]),
                                  ALU.subtract).then_inc(sub_ok, 1)

            def second_var():
                dve.wait_ge(mv2_ok, NT)
                dve.tensor_scalar(ve2[:], mv2[:, :, 1], EPS, None, ALU.add).then_inc(var2_ok, 1)

            def second_norm():
                dve.wait_ge(rstd2_ok, 1)
                for m in range(NT):
                    i = dve.tensor_scalar(xn2[:, m], x2[:, m], mv2[:, m, 0:1], rstd2[:, m:m + 1],
                                          ALU.subtract, ALU.mult)
                i.then_inc(xn2_ok, 1)

            def take_logits():
                dve.tensor_tensor(lg[:], bank[7][:, 0:NT * 8].rearrange("p (m e) -> p m e", e=8)[:, :, 0:7],
                                  rb_b[:].unsqueeze(1).broadcast_to([P, NT, 7]), ALU.add).then_inc(lg_ok, 1)

            b7 = lambda a: a.unsqueeze(2).broadcast_to([P, NT, 7])
            m1, m2, dif, edif, den, w1, w2, v = (rs[:, i] for i in range(8))

            def pick_expert(top, pick, k):
                def step(i, ins):
                    ins.then_inc(rt_ok, 1)
                    dve.wait_ge(rt_ok, 5 * k + i)

                first = firstof[:].unsqueeze(1).broadcast_to([P, NT, 7])
                dve.wait_ge(lg_ok, k + 1)
                step(1, dve.tensor_reduce(top, lg[:], AX.X, ALU.max))
                step(2, dve.tensor_tensor(lt[:], lg[:], b7(top), ALU.is_equal))
                step(3, dve.tensor_tensor(lt[:], lt[:], first, ALU.mult))
                step(4, dve.tensor_reduce(v, lt[:], AX.X, ALU.max))
                step(5, dve.tensor_tensor(pick[:], lt[:], b7(v), ALU.is_equal))

            def first_expert():
                pick_expert(m1, oh1, 0)
                dve.scalar_tensor_tensor(lg[:], oh1[:], -BIG, lg[:], ALU.mult, ALU.add).then_inc(lg_ok, 1)

            def second_expert():
                pick_expert(m2, oh2, 1)
                dve.tensor_tensor(dif, m2, m1, ALU.subtract).then_inc(dif_ok, 1)

            def expert_weights():
                dve.wait_ge(edif_ok, 1)
                dve.tensor_scalar(den, edif, 1.0, 2.0, ALU.add, ALU.mult).then_inc(w_ok, 1)
                dve.wait_ge(w_ok, 1)
                dve.reciprocal(w1, den).then_inc(w_ok, 1)
                dve.wait_ge(w_ok, 2)
                dve.tensor_tensor(w2, edif, w1, ALU.mult).then_inc(w_ok, 1)
                dve.tensor_tensor(oh1[:], oh1[:], b7(w1), ALU.mult).then_inc(w_ok, 1)
                dve.wait_ge(w_ok, 4)
                dve.tensor_tensor(oh2[:], oh2[:], b7(w2), ALU.mult).then_inc(w_ok, 1)
                dve.wait_ge(w_ok, 5)
                dve.tensor_tensor(W[:, :, 1:8], oh1[:], oh2[:], ALU.add).then_inc(w_ok, 1)
                dve.wait_ge(w_ok, 6)
                dve.tensor_copy(whi[:], W[:]).then_inc(w_ok, 1)
                dve.wait_ge(w_ok, 7)
                dve.tensor_copy(W16[:, :, 0:8], whi[:].bitcast(F32))
                dve.tensor_tensor(W16[:, :, 8:16], W[:], whi[:].bitcast(F32), ALU.subtract).then_inc(var_w, 1)

            def weigh(e):
                dve.wait_ge(y_ps, e + 1)
                dve.wait_ge(wB_ok, e + 1)
                if e >= 1:
                    dve.wait_ge(acc_ok, e)
                dve.tensor_tensor(yw, bank[4][:], wB[:, e % 2], ALU.mult).then_inc(yw_ok, 1)

            def hidden(n):
                w = CH[n % 3][1]
                dve.wait_ge(t_ok, n + 1)
                dve.scalar_tensor_tensor(ag[0:w, n % 2], tg[0:w, n % 2], 1.0, bank[n % 2][0:w, :],
                                         ALU.add, ALU.mult).then_inc(a_ok, 1)
                dve.wait_ge(a_ok, n + 1)
                dve.wait_ge(u_ps, n + 1)
                if n >= 2:
                    dve.wait_ge(lo_ok, n - 1)
                dve.tensor_tensor(hg[0:w, n % 2], ag[0:w, n % 2], bank[2 + n % 2][0:w, :],
                                  ALU.mult).then_inc(h_ok, 1)

            def finish(k):
                dve.wait_ge(fT_ps, k)
                if k > 1:
                    dve.wait_ge(keep_ok, 1)
                    dve.wait_ge(out_done, 16)
                dve.scalar_tensor_tensor(fin, bank[4][:].rearrange("p (m d) -> p m d", m=NT), tgate[:, 1:2],
                                         x2keep, ALU.mult, ALU.add).then_inc(fin_ok, 1)

            def attend(n):
                if n == 3:
                    choose()
                if n == 4:
                    value_bias(0)
                if n == 5:
                    query_mask()
                if n == 6:
                    value_bias(1)
                if n in SCORES_AT:
                    softmax_shift(SCORES_AT[n])
                if n in PROJECT_AT:
                    residual(PROJECT_AT[n])
                if n == 22:
                    second_var()

            def iteration(experts, attention, finishing):
                if experts:
                    take_logits()
                for n in range(NS):
                    if attention and n == 0:
                        first_stats()
                    if attention and n in NORMALISE_AT:
                        normalise(NORMALISE_AT[n])
                    if experts:
                        if n in WEIGH_AT:
                            weigh(WEIGH_AT[n])
                        if attention and n == NS - 1:
                            second_norm()
                        hidden(n)
                        if n == 1:
                            if finishing:
                                finish(1)
                                dve.wait_ge(fin_ok, 1)
                            dve.tensor_copy(x2keep, x2[:]).then_inc(keep_ok, 1)
                        if n == 2:
                            first_expert()
                        if n == 4:
                            second_expert()
                        if n == 5:
                            expert_weights()
                    elif n == NS - 1:
                        second_norm()
                    if attention and n == 0:
                        first_norm()
                    if attention:
                        if not experts and n == 1:
                            masks()
                        attend(n)
                if experts:
                    weigh(E - 1)
                if attention:
                    dve.wait_ge(xhi_ok, 1)
                    dve.tensor_tensor(xlo[:], bank[6][:], xhi[:].bitcast(F32), ALU.subtract).then_inc(xlo_ok, 1)

            once()
            dve.wait_ge(x_in, 16)
            iteration(False, True, False)
            meet(dve)
            iteration(True, True, False)
            meet(dve)
            with dve.Fori(2, NG):
                iteration(True, True, True)
                meet(dve)
            iteration(True, False, True)
            finish(2)

        @block.tensor
        def _(pe):
            def values(hv):
                if hv:
                    pe.wait_ge(vtmp_ok, 1)
                else:
                    pe.wait_ge(k_ok, 4)
                for b in range(4):
                    i = pe.matmul(bank[7][:, b * D:(b + 1) * D],
                                  ctx[:, hv * 4 + b].rearrange("p a l -> p (a l)"), wv_sb[:],
                                  start=True, stop=True)
                i.then_inc(v_ps, 1)

            def scores(b):
                pe.wait_ge(qexp_ok, b + 1)
                if b == 0:
                    pe.wait_ge(mask_ok, 1)
                else:
                    pe.wait_ge(sub_ok, b)
                for pp in range(2):
                    dst = bank[5][:].rearrange("p (j x k) -> p j x k", j=4, x=2)[:, :, pp]
                    pair = slice(2 * pp, 2 * pp + 2)
                    pe.matmul(dst, qexp[:, b, pair], kquad[:, :, b * L:(b + 1) * L],
                              start=True, stop=False)
                    i = pe.matmul(dst, quadpick[:, b, pair].rearrange("p a l -> p (a l)"),
                                  keybias[:], start=False, stop=True)
                i.then_inc(s_ps, 1)

            def prob_transposes(b):
                pe.wait_ge(exp_ok, b + 1)
                if b == 0:
                    pe.wait_ge(selP_ok, 2)
                else:
                    pe.wait_ge(pT_ok, b)
                for j in range(4):
                    i = pe.transpose(bank[6][:, j * P:(j + 1) * P],
                                     prob[:, b % 2, 2 * j:2 * j + 2].rearrange("p a k -> p (a k)"), ident[:])
                i.then_inc(pT_ps, 1)

            def context(b):
                pe.wait_ge(pT_ok, b + 1)
                pe.wait_ge(vblk_ok, 2 * (b // 4) + 2)
                if b == 0:
                    pe.wait_ge(vtmp_ok, 2)
                elif b % 2 == 0:
                    pe.wait_ge(x2_ok, b // 2)
                r = slice(64 * (b % 2), 64 * (b % 2) + 64)
                for n in range(8):
                    i = pe.matmul(bank[7][r, n * 2 * VW:(n + 1) * 2 * VW], probT[:, b % 2, n * 64:(n + 1) * 64],
                                  vblk[:, b * 8 + n].rearrange("p x v -> p (x v)"), start=True, stop=True)
                i.then_inc(pv_ps, 1)

            def ctx_transpose(m):
                pe.wait_ge(cn_ok, m + 1)
                pe.transpose(bank[7][:, 0:D], cn[:, m % 2], ident[:]).then_inc(cT_ps, 1)

            def project(m):
                pe.wait_ge(cT_ok, m + 1)
                pe.matmul(bank[7][:, 0:D], cnT[:, m % 2], wo_sb[:], start=True, stop=True).then_inc(o_ps, 1)

            def second_transposes():
                pe.wait_ge(xn2_ok, 1)
                pe.wait_ge(pT_ok, GB)
                for m in range(NT):
                    i = pe.transpose(bank[6][:, m * P:(m + 1) * P], xn2[:, m], ident[:])
                i.then_inc(xn2T_ps, 1)

            def logits():
                pe.wait_ge(xlo_ok, 1)
                for m in range(NT):
                    t = slice(m * P, (m + 1) * P)
                    for k, (a, b) in enumerate(((xhi, wr_hi), (xhi, wr_lo), (xlo, wr_hi))):
                        i = pe.matmul(bank[7][:, m * 8:(m + 1) * 8], a[:, t], b[:], start=k == 0, stop=k == 2)
                i.then_inc(lg_ps, 1)

            def weight_transposes():
                pe.wait_ge(var_w, 1)
                for m in range(NT):
                    i = pe.transpose(bank[4][0:16, m * P:(m + 1) * P], W16[:, m], ident[:])
                i.then_inc(wT_ps, 1)

            def spread_weight(e):
                if e == 0:
                    pe.wait_ge(wT_ok, 1)
                else:
                    pe.wait_ge(yw_ok, e)
                pe.matmul(bank[4][:], pick16[:, e], WT[:], start=True, stop=True).then_inc(wB_ps, 1)

            def gate_up(n):
                e, c = n // 3, n % 3
                c0, w = CH[c]
                if n >= 2:
                    pe.wait_ge(h_ok, n - 1)
                for part, (bk_, sem_) in enumerate(((n % 2, g_ps), (2 + n % 2, u_ps))):
                    o = (e * 2 + part) * I + c0
                    for k, (wt, xx) in enumerate(((gu_hi, xhi), (gu_hi, xlo), (gu_lo, xhi))):
                        i = pe.matmul(bank[bk_][0:w, :], wt[:, o:o + w], xx[:], start=k == 0, stop=k == 2)
                    i.then_inc(sem_, 1)

            def down(e, between=None):
                pe.wait_ge(wB_ok, e + 1)
                for c in range(3):
                    pe.wait_ge(lo_ok, 3 * e + c + 1)
                    if between is not None and c == 2:
                        between()
                    w = CH[c][1]
                    sl = (3 * e + c) % HS
                    for k, (wt, hh) in enumerate(((wd_hi, h_hi), (wd_hi, h_lo), (wd_lo, h_hi))):
                        i = pe.matmul(bank[4][:], wt[0:w, c, e * D:(e + 1) * D], hh[0:w, sl],
                                      start=c == 0 and k == 0, stop=c == 2 and k == 2)
                i.then_inc(y_ps, 1)

            def sum_transposes(k):
                if k > 1:
                    pe.wait_ge(acc_ok, E)
                for m in range(NT):
                    i = pe.transpose(bank[4][:, m * P:(m + 1) * P], acc[:, m * P:(m + 1) * P], ident[:])
                i.then_inc(fT_ps, 1)

            def attend(n):
                if n == 1:
                    pe.wait_ge(xn_ok, 1)
                    for m in range(NT):
                        i = pe.transpose(bank[5][:, m * P:(m + 1) * P], xn[:, m], ident[:])
                    i.then_inc(xnT_ps, 1)
                    pe.matmul(bank[7][:], wk_sb[:], ctx[:, :, 0], start=True, stop=True).then_inc(k_ps, 1)
                if n == 2:
                    pe.wait_ge(xnT_ok, 1)
                    pe.matmul(bank[6][:], wq_sb[:], xnT[:], start=True, stop=True).then_inc(q_ps, 1)
                if n == 3:
                    pe.wait_ge(qsq_ok, 1)
                    for b in range(GB):
                        i = pe.matmul(bank[5][:, 0:L], headsum[:, b], qsq[:, b * L:(b + 1) * L],
                                      start=b == 0, stop=b == GB - 1)
                    i.then_inc(norm_ps, 1)
                    values(0)
                if n == 5:
                    pe.wait_ge(seld_ok, 1)
                    pe.transpose(bank[6][:, 0:P], seld[:].rearrange("p a l -> p (a l)"),
                                 ident[:]).then_inc(selT_ps, 1)
                    values(1)
                if n in SCORES_AT:
                    scores(SCORES_AT[n])
                if n in CONTEXT_AT:
                    context(2 * CONTEXT_AT[n])
                    context(2 * CONTEXT_AT[n] + 1)
                if n in NORMALISE_AT:
                    ctx_transpose(NORMALISE_AT[n])
                if n in PROJECT_AT:
                    project(PROJECT_AT[n])
                if n in TRANSPOSE_AT:
                    prob_transposes(TRANSPOSE_AT[n])

            def iteration(experts, attention, finishing):
                for n in range(NS):
                    if experts:
                        gate_up(n)
                        if n == 0 and finishing:
                            sum_transposes(1)
                        if n == WT_AT:
                            if finishing:
                                pe.wait_ge(fin_ok, 1)
                            weight_transposes()
                        if n in SPREAD_AT:
                            spread_weight(SPREAD_AT[n])
                        if n in DOWN_AT:
                            down(DOWN_AT[n])
                    if attention:
                        if experts and n == 1:
                            pe.wait_ge(lg_ok, 1)
                        if not experts:
                            if n == 3:
                                pe.wait_ge(c_masks, 1)
                            if n == 8:
                                pe.wait_ge(c_zero, 11)
                        attend(n)
                if experts:
                    spread_weight(E - 1)
                    down(E - 1, second_transposes if attention else None)
                elif attention:
                    second_transposes()
                if attention:
                    logits()

            pe.wait_ge(c_ident, 1)
            pe.wait_ge(wqkv_in, 64)
            pe.wait_ge(ctx_in, 32)
            pe.wait_ge(wr_ok, 2)
            iteration(False, True, False)
            meet(pe)
            pe.wait_ge(pick_ok, 1)
            pe.wait_ge(wgt_lo, GUP + NC_)
            iteration(True, True, False)
            meet(pe)
            with pe.Fori(2, NG):
                iteration(True, True, True)
                meet(pe)
            iteration(True, False, True)
            pe.wait_ge(yw_ok, E)
            sum_transposes(2)


def kernel(**inputs):
    import numpy as np
    import concourse.bacc as bacc
    from concourse import mybir as _mybir
    from concourse.bass_utils import run_bass_kernel_spmd as run

    a = {k: np.asarray(v) for k, v in inputs.items()}
    heads = np.arange(D).reshape(4, 2, 2, DK).transpose(0, 2, 1, 3).reshape(-1)
    gate = np.concatenate([a["L0_ffn_sg"][None], a["L0_ffn_rg"]])
    up = np.concatenate([a["L0_ffn_su"][None], a["L0_ffn_ru"]])
    down = np.concatenate([a["L0_ffn_sd"][None], a["L0_ffn_rd"]])
    arrays = {
        "x": a["x"].reshape(B * L, D),
        "ctxT": a["ctx_1024"].reshape(B * L, D).T,
        "gates": np.concatenate([a["g_xattn"], a["g_ffn"]]),
        "wq": a["L0_xattn_Wq"], "bq": a["L0_xattn_bq"], "wk": a["L0_xattn_Wk"], "bk": a["L0_xattn_bk"],
        "wv": a["L0_xattn_Wv"], "bv": a["L0_xattn_bv"], "wo": a["L0_xattn_Wo"][heads], "bo": a["L0_xattn_bo"],
        "wgu": np.stack([gate, up], 1).transpose(3, 0, 1, 2).reshape(D, -1),
        "wd": down.transpose(0, 2, 1),
        "wrT": a["L0_ffn_wr"].T, "rb": a["L0_ffn_rb"],
    }
    arrays = {k: np.ascontiguousarray(v) for k, v in arrays.items()}
    nc = bacc.Bacc("TRN2", target_bir_lowering=False, num_devices=1)
    args = [nc.dram_tensor(f"in_{k}", v.shape, _mybir.dt.from_np(v.dtype), kind="ExternalInput").ap()
            for k, v in arrays.items()]
    y = nc.dram_tensor("out_y", (B * L, D), _mybir.dt.float32, kind="ExternalOutput").ap()
    gated_block(nc, *args, y)
    r = run(nc, [{f"in_{k}": v for k, v in arrays.items()}], core_ids=[0])
    return r.results[0]["out_y"].reshape(B, L, D)
```

```python
from contextlib import ExitStack

import concourse.bass as bass
from concourse import mybir

F32 = mybir.dt.float32
F32R = mybir.dt.float32r
BF16 = mybir.dt.bfloat16
ALU = mybir.AluOpType
ACT = mybir.ActivationFunctionType
AX = mybir.AxisListType

P = 128
D = 128
B, L = 64, 64
H, DK = 16, 8
U = L // 2
I = 352
E = 8
GB = 8
NG = B // GB
GT = GB * L
NT = GT // P
CH = [(0, 128), (128, 128), (256, 96)]
NC_ = len(CH)
NS = E * NC_
HS = 8
VW = DK + 1
assert U % 8 == 0 and U // 8 == 4
def stages(batch_at, context_at, ahead, keys, values_at, score_banks, context_banks):
    scores = {batch_at(b): b for b in range(GB)}
    context = {context_at(m): m for m in range(NT)}
    return {"keys": keys, "values": {values_at: 0, values_at + 2: 1},
            "spread": {values_at + 1: 0, values_at + 3: 1},
            "score_banks": score_banks, "context_banks": context_banks,
            "queries": {n - ahead: b for n, b in scores.items()}, "scores": scores,
            "transposes": {n + 1: b for n, b in scores.items()}, "probs": {n + 2: b for n, b in scores.items()},
            "context": context, "normalise": {n + 1: m for n, m in context.items()},
            "project": {n + 2: m for n, m in context.items()}}


BESIDE = stages(lambda b: 8 + 3 * (b // 2) + b % 2, lambda m: 11 + 3 * m, 3, {3 + j: (j,) for j in range(4)}, 7,
                (5,), (7,))
ALONE = stages(lambda b: 8 + b, lambda m: 11 + 2 * m, 5, {3: range(4)}, 4,
               (5, 4), (7, 3))
DOWN_AT = {8: 0, 10: 1, 12: 2, 14: 3, **{3 * e + 4: e for e in range(4, E - 1)}}
SPREAD_AT = {n - 1: e for n, e in DOWN_AT.items()}
WEIGH_AT = {n + 1: e for n, e in DOWN_AT.items()}
PICK_AT = 1
WT_AT = 7
CHOOSE_AT = 3
LATE = (slice(0, NT - 1), slice(NT - 1, NT))
SECOND_VAR_AT = {20: 0, 22: 1}
GUP = 8
SPLIT_AT = {8 + k: k for k in range(GUP + NC_)}
BIG = 1e30
HUGE = 1e38
EPS = 1e-5
SCALE = float(DK) ** -0.5


def gated_block(nc, x, ctxT, gates, wq, bq, wk, bk, wv, bv, wo, bo, wgu, wd, wrT, rb, out):
    st = ExitStack()
    with st:
        def sb(name, shape, dt=F32):
            return st.enter_context(nc.sbuf_tensor(name, shape, dt))

        def sem(name):
            return st.enter_context(nc.semaphore(name))

        bank = [st.enter_context(nc.psum_tensor(f"bank{i}", [P, 512], F32)) for i in range(8)]

        ident = sb("ident", [P, P])
        quadpick = sb("quadpick", [P, GB, 4, L], BF16)
        picked = sb("picked", [P, GB, 4])
        quadmask = sb("quadmask", [P, 4])
        headsum = sb("headsum", [P, GB, P])
        rowmask = sb("rowmask", [P, 4])
        halfmask = sb("halfmask", [P, 2])
        pick16 = sb("pick16", [16, E, P], F32R)
        negh = sb("negh", [P, NT])
        wq_sb, wk_sb, wv_sb, wo_sb = (sb(n, [P, D]) for n in ("wq_sb", "wk_sb", "wv_sb", "wo_sb"))
        bqk = sb("bqk", [P, 2])
        bv_b = sb("bv_b", [P, D])
        bv_rest = sb("bv_rest", [P, D])
        bv_part = sb("bv_part", [P, 3, D], BF16)
        bv_parts = sb("bv_parts", [P, D], BF16)
        ones = sb("ones", [P, P], BF16)
        bo_b = sb("bo_b", [P, D])
        tbo = sb("tbo", [P, D])
        rb_b = sb("rb_b", [P, E])
        gate_in = sb("gate_in", [P, 2])
        tgate = sb("tgate", [P, 2])
        wr_sb = sb("wr_sb", [P, 8])
        wr_hi = sb("wr_hi", [P, 8], F32R)
        wr_lo = sb("wr_lo", [P, 8], F32R)
        GUW = E * 2 * I
        gu_hi = sb("gu_hi", [P, GUW], F32R)
        gu_lo = sb("gu_lo", [P, GUW], F32R)
        wd_hi = sb("wd_hi", [P, NC_, E * D], F32R)
        wd_lo = sb("wd_lo", [P, NC_, E * D], F32R)

        xg = sb("xg", [P, NT, D])
        xpb = sb("xpb", [P, NT, D])
        x2 = sb("x2", [P, NT, D])
        ctx = sb("ctx", [P, GB, 2, L])
        stats = sb("stats", [P, NT, 6])
        mv = sb("mv", [P, NT, 2])
        ve = sb("ve", [P, NT])
        rstd = sb("rstd", [P, NT])
        stats2 = sb("stats2", [P, NT, 6])
        mv2 = sb("mv2", [P, NT, 2])
        ve2 = sb("ve2", [P, NT])
        rstd2 = sb("rstd2", [P, NT])
        xn = sb("xn", [P, NT, D])
        xnT = sb("xnT", [P, GT])
        q = sb("q", [P, GT])
        qsq = xnT
        qexp = sb("qexp", [P, GB, 4, L])
        kquad = sb("kquad", [P, 4, GT])
        top8 = sb("top8", [P, 4, 8])
        rest = sb("rest", [P, 4, L])
        keybias = sb("keybias", [P, 4, L], BF16)
        bias = sb("bias", [P, L])
        seld = sb("seld", [P, 2, L])
        selP = sb("selP", [P, NT, H])
        vblk = sb("vblk", [P, GB * 8, 2, VW])
        mx = sb("mx", [P, 2, 8])
        prob = sb("prob", [P, 2, 8, L])
        pick16f = prob[0:16].rearrange("p s a k -> p (s a k)").rearrange("p (e n) -> p e n", e=E)
        probT = sb("probT", [P, 2, 512])
        rec = sb("rec", [P, 2, H])
        recs = sb("recs", [P, 2, H])
        cn = sb("cn", [P, 2, D])
        cnT = sb("cnT", [P, 2, D])
        xn2 = xn
        xhi = sb("xhi", [P, GT], F32R)
        xlo = sb("xlo", [P, GT], F32R)
        lg = sb("lg", [P, NT, 8])
        ltop = sb("ltop", [P, NT, 8])
        ltwo = sb("ltwo", [P, NT, 8])
        lmark = sb("lmark", [P, NT, 8])
        ldif = sb("ldif", [P, NT, 8])
        lpick = sb("lpick", [P, NT, 8])
        lsum = sb("lsum", [P, NT])
        lrec = sb("lrec", [P, NT])
        W = sb("W", [P, NT, 8])
        W16 = sb("W16", [P, NT, 16])
        whi = sb("whi", [P, NT, 8], F32R)
        WT = sb("WT", [16, GT], F32R)
        work = sb("work", [P, 6144])
        wB = work[:, 0:1024].rearrange("p (s t) -> p s t", s=2)
        acc = work[:, 1024:1536]
        yw = work[:, 1536:2048]
        lgT = qexp[0:8, 0:2].rearrange("p b r l -> p (b r l)")
        fin = work[:, 2048:2560].rearrange("p (m d) -> p m d", m=NT)
        x2keep = work[:, 2560:3072].rearrange("p (m d) -> p m d", m=NT)
        tg = work[:, 3072:4096].rearrange("p (s t) -> p s t", s=2)
        ag = work[:, 4096:5120].rearrange("p (s t) -> p s t", s=2)
        hg = work[:, 5120:6144].rearrange("p (s t) -> p s t", s=2)
        h_hi = sb("h_hi", [P, HS, GT], F32R)
        h_lo = sb("h_lo", [P, HS, GT], F32R)

        small_in = sem("small_in")
        wqkv_in = sem("wqkv_in")
        c_ident = sem("c_ident")
        c_gp = sem("c_gp")
        c_masks = sem("c_masks")
        c_zero = sem("c_zero")
        c_pick = sem("c_pick")
        rowmask_ok = sem("rowmask_ok")
        pick_ok = sem("pick_ok")
        tgate_ok = sem("tgate_ok")
        tbo_ok = sem("tbo_ok")
        wr_ok = sem("wr_ok")
        gu_in = [sem(f"gu_in{k}") for k in range(GUP)]
        wd_in = [sem(f"wd_in{c}") for c in range(NC_)]
        bv_split = sem("bv_split")
        bv_ok = sem("bv_ok")
        wgt_hi = sem("wgt_hi")
        wgt_lo = sem("wgt_lo")
        x_in = sem("x_in")
        ctx_in = sem("ctx_in")
        out_done = sem("out_done")
        bn_ok = sem("bn_ok")
        mv_ok = sem("mv_ok")
        var_ok = sem("var_ok")
        rstd_ok = sem("rstd_ok")
        xn_ok = sem("xn_ok")
        xpb_ok = sem("xpb_ok")
        xnT_ps = sem("xnT_ps")
        xnT_ok = sem("xnT_ok")
        q_ps = sem("q_ps")
        k_ps = sem("k_ps")
        q_ok = sem("q_ok")
        k_ok = sem("k_ok")
        qsq_ok = sem("qsq_ok")
        qexp_ok = sem("qexp_ok")
        norm_ps = sem("norm_ps")
        top_ok = sem("top_ok")
        bias_ok = sem("bias_ok")
        mask_ok = sem("mask_ok")
        seld_ok = sem("seld_ok")
        selT_ps = sem("selT_ps")
        selP_ok = sem("selP_ok")
        v_ps = sem("v_ps")
        vblk_ok = sem("vblk_ok")
        s_ps = sem("s_ps")
        mx_ok = sem("mx_ok")
        sub_ok = sem("sub_ok")
        exp_ok = sem("exp_ok")
        pT_ps = sem("pT_ps")
        pT_ok = sem("pT_ok")
        pv_ps = sem("pv_ps")
        rec_ok = sem("rec_ok")
        recs_ok = sem("recs_ok")
        cn_ok = sem("cn_ok")
        cT_ps = sem("cT_ps")
        cT_ok = sem("cT_ok")
        o_ps = sem("o_ps")
        x2_ok = sem("x2_ok")
        bn2_ok = sem("bn2_ok")
        mv2_ok = sem("mv2_ok")
        var2_ok = sem("var2_ok")
        rstd2_ok = sem("rstd2_ok")
        xn2_ok = sem("xn2_ok")
        xn2T_ps = sem("xn2T_ps")
        xhi_ok = sem("xhi_ok")
        lg_ps = sem("lg_ps")
        last_ok = sem("last_ok")
        lo_last = sem("lo_last")
        lgT_ps = sem("lgT_ps")
        lgT_ok = sem("lgT_ok")
        lg_ok = sem("lg_ok")
        rt_ok = sem("rt_ok")
        dif_ok = sem("dif_ok")
        exps_ok = sem("exps_ok")
        w_ok = sem("w_ok")
        var_w = sem("var_w")
        wT_ps = sem("wT_ps")
        wT_ok = sem("wT_ok")
        wB_ps = sem("wB_ps")
        wB_ok = sem("wB_ok")
        g_ps = sem("g_ps")
        u_ps = sem("u_ps")
        t_ok = sem("t_ok")
        a_ok = sem("a_ok")
        h_ok = sem("h_ok")
        hi_ok = sem("hi_ok")
        lo_ok = sem("lo_ok")
        y_ps = sem("y_ps")
        yw_ok = sem("yw_ok")
        acc_ok = sem("acc_ok")
        fT_ps = sem("fT_ps")
        keep_ok = sem("keep_ok")
        fin_ok = sem("fin_ok")

        arrived = sem("arrived")
        go = {e.engine: sem(f"go_{n}") for n, e in (("sync", nc.sync), ("scalar", nc.scalar), ("vector", nc.vector),
                                                     ("tensor", nc.tensor))}

        block = st.enter_context(nc.Block())
        counted = range(x_in.num, fin_ok.num + 1)

        def meet(eng):
            eng.drain().then_inc(arrived, 1)
            eng.wait_ge(go[eng.engine], 1)
            eng.sem_inc(go[eng.engine], -1)

        def meet_pool(gp):
            gp.drain()
            gp.wait_ge(arrived, 4)
            gp.sem_inc(arrived, -4)
            gp.sem_clear(counted)
            for sem_ in go.values():
                gp.sem_inc(sem_, 1)

        def raw_weights(k):
            w = GUW // GUP
            if k < GUP:
                return work[:, k * w:(k + 1) * w]
            c = k - GUP
            return work[0:CH[c][1], c * E * D:(c + 1) * E * D]

        def split_weights(k, gate_up, down):
            if k < GUP:
                return gate_up[:, k * GUW // GUP:(k + 1) * GUW // GUP]
            return down[0:CH[k - GUP][1], k - GUP]

        def turn(banks, k):
            return bank[banks[k % len(banks)]]

        x_v = x.rearrange("(t p) d -> p t d", p=P)
        out_v = out.rearrange("(t p) d -> p t d", p=P)

        @block.sync
        def _(sp):
            def load_x(g):
                sp.dma_start(xg[:], x_v[:, bass.ds(g * NT, NT), :]).then_inc(x_in, 16)

            def load_ctx(g):
                src = ctxT[:, bass.ds(g * GT, GT)].rearrange("p (b l) -> p b l", b=GB)
                for twice in range(2):
                    sp.dma_start(ctx[:, :, twice], src).then_inc(ctx_in, 16)

            def next_group(g):
                sp.wait_ge(xn_ok, 1)
                sp.wait_ge(xpb_ok, 1)
                load_x(g)
                sp.wait_ge(k_ps, 1)
                sp.wait_ge(v_ps, 2)
                load_ctx(g)

            def store(g):
                sp.wait_ge(fin_ok, 1)
                sp.dma_start(out_v[:, bass.ds(g * NT, NT), :], fin).then_inc(out_done, 16)

            def landed():
                sp.wait_ge(x_in, 16)
                sp.wait_ge(ctx_in, 32)

            load_x(0)
            for dst, src in ((wq_sb, wq), (wk_sb, wk), (wv_sb, wv), (wo_sb, wo)):
                sp.dma_start(dst[:], src).then_inc(wqkv_in, 16)
            load_ctx(0)
            for dst, src in ((bqk[:, 0:1], bq.unsqueeze(1)), (bqk[:, 1:2], bk.unsqueeze(1)),
                             (wr_sb[:, 0:7], wrT),
                             (bv_b[:], bv.unsqueeze(0).broadcast_to([P, D])),
                             (bo_b[:], bo.unsqueeze(0).broadcast_to([P, D])),
                             (rb_b[:, 0:7], rb.unsqueeze(0).broadcast_to([P, 7])),
                             (gate_in[:], gates.unsqueeze(0).broadcast_to([P, 2]))):
                sp.dma_start(dst, src).then_inc(small_in, 16)
            for k in range(GUP):
                sp.dma_start(raw_weights(k), wgu[:, k * GUW // GUP:(k + 1) * GUW // GUP]).then_inc(gu_in[k], 16)
            next_group(1)
            for c, (c0, w) in enumerate(CH):
                sp.wait_ge(wgt_lo, -(-(c + 1) * E * D // (GUW // GUP)))
                sp.dma_start(raw_weights(GUP + c).rearrange("p (e h) -> p e h", e=E),
                             wd[:, c0:c0 + w, :].rearrange("e i h -> i e h")).then_inc(wd_in[c], 16)
            sp.wait_ge(x_in, 32)
            sp.wait_ge(ctx_in, 64)
            meet(sp)
            next_group(2)
            landed()
            meet(sp)
            with sp.Fori(2, NG - 1) as g:
                store(g - 2)
                next_group(g + 1)
                landed()
                sp.wait_ge(out_done, 16)
                meet(sp)
            store(NG - 3)
            sp.wait_ge(out_done, 16)
            meet(sp)
            store(NG - 2)
            sp.wait_ge(fin_ok, 2)
            sp.dma_start(out_v[:, (NG - 1) * NT:NG * NT, :], fin).then_inc(out_done, 16)
            sp.wait_ge(out_done, 32)

        @block.gpsimd
        def _(gp):
            gp.memset(ident[:], 0.0).then_inc(c_gp, 1)
            gp.memset(negh[:], -0.5).then_inc(c_gp, 1)
            gp.memset(wr_sb[:, 7:8], 0.0).then_inc(c_gp, 1)
            gp.wait_ge(c_gp, 3)
            gp.affine_select(out=ident[:], in_=ident[:], compare_op=ALU.not_equal, fill=1.0, base=0,
                             pattern=[[-1, P]], channel_multiplier=1).then_inc(c_ident, 1)

            def sum_mask():
                gp.memset(headsum[:], 1.0).then_inc(c_gp, 1)
                gp.wait_ge(c_gp, 4)
                gp.affine_select(out=headsum[:], in_=headsum[:], compare_op=ALU.is_ge, fill=0.0, base=0,
                                 pattern=[[P, GB], [-DK, P]], channel_multiplier=1).then_inc(c_gp, 1)
                gp.wait_ge(c_gp, 5)
                gp.affine_select(out=headsum[:], in_=headsum[:], compare_op=ALU.is_ge, fill=0.0, base=DK - 1,
                                 pattern=[[-P, GB], [DK, P]], channel_multiplier=-1).then_inc(c_masks, 1)

            def router_masks():
                gp.memset(pick16f, 0.0).then_inc(c_gp, 1)
                gp.memset(rb_b[:, 7:8], -BIG).then_inc(c_gp, 1)
                gp.memset(ltwo[:], -3 * HUGE).then_inc(c_gp, 1)
                gp.wait_ge(c_gp, 8)
                gp.affine_select(out=pick16f, in_=pick16f, compare_op=ALU.not_equal, fill=1.0, base=0,
                                 pattern=[[-1, E], [0, P]], channel_multiplier=1).then_inc(c_gp, 1)
                gp.wait_ge(c_gp, 9)
                gp.affine_select(out=pick16f, in_=pick16f, compare_op=ALU.not_equal, fill=1.0, base=-E,
                                 pattern=[[-1, E], [0, P]], channel_multiplier=1).then_inc(c_pick, 1)

            def expand_queries(b):
                gp.tensor_tensor(
                    qexp[:, b], q[:, b * L:(b + 1) * L].unsqueeze(1).broadcast_to([P, 4, L]),
                    rowmask[:].unsqueeze(2).broadcast_to([P, 4, L]), ALU.mult).then_inc(qexp_ok, 1)

            def attend(n, at):
                if n == 0:
                    gp.wait_ge(var_ok, 1)
                    gp.tensor_tensor(rstd[:], ve[:], negh[:], ALU.pow).then_inc(rstd_ok, 1)
                if n == 1:
                    gp.wait_ge(tbo_ok, 1)
                    gp.tensor_tensor(xpb[:], xg[:], tbo[:].unsqueeze(1).broadcast_to([P, NT, D]),
                                     ALU.add).then_inc(xpb_ok, 1)
                if n == 2:
                    gp.wait_ge(q_ok, 1)
                    gp.wait_ge(rowmask_ok, 1)
                if n in at["queries"]:
                    expand_queries(at["queries"][n])
                if n in SECOND_VAR_AT:
                    k = SECOND_VAR_AT[n]
                    gp.wait_ge(var2_ok, k + 1)
                    gp.tensor_tensor(rstd2[:, LATE[k]], ve2[:, LATE[k]], negh[:, LATE[k]],
                                     ALU.pow).then_inc(rstd2_ok, 1)

            def weights_lo(k):
                gp.wait_ge(wgt_hi, k + 1)
                gp.tensor_tensor(split_weights(k, gu_lo, wd_lo), raw_weights(k),
                                 split_weights(k, gu_hi, wd_hi).bitcast(F32), ALU.subtract).then_inc(wgt_lo, 1)

            def lo_part(n):
                w = CH[n % 3][1]
                gp.wait_ge(hi_ok, n + 1)
                gp.tensor_tensor(h_lo[0:w, n % HS], hg[0:w, n % 2], h_hi[0:w, n % HS].bitcast(F32),
                                 ALU.subtract).then_inc(lo_ok, 1)

            def add_expert(e):
                gp.wait_ge(yw_ok, e + 1)
                if e == 0:
                    gp.tensor_copy(acc, yw).then_inc(acc_ok, 1)
                else:
                    gp.wait_ge(acc_ok, e)
                    gp.tensor_tensor(acc, acc, yw, ALU.add).then_inc(acc_ok, 1)

            def iteration(experts, attention, finishing=False):
                at = BESIDE if experts else ALONE
                for n in range(NS):
                    if finishing and n == 0:
                        gp.tensor_tensor(acc, acc, yw, ALU.add).then_inc(last_ok, 1)
                    if attention and n == 0:
                        attend(0, at)
                        if not experts:
                            router_masks()
                    if experts and n >= 1:
                        lo_part(n - 1)
                    if experts and n in WEIGH_AT:
                        add_expert(WEIGH_AT[n])
                    if attention and n > 0:
                        attend(n, at)
                    if not experts and n in SPLIT_AT:
                        weights_lo(SPLIT_AT[n])

            sum_mask()
            iteration(False, True)
            meet_pool(gp)
            iteration(True, True)
            meet_pool(gp)
            with gp.Fori(2, NG):
                iteration(True, True, True)
                meet_pool(gp)
            iteration(True, False, True)


        @block.scalar
        def _(act):
            act.wait_ge(small_in, 16 * 7)
            act.activation(tgate[:], gate_in[:], ACT.Tanh).then_inc(tgate_ok, 1)

            def weights_hi(k):
                act.wait_ge(gu_in[k] if k < GUP else wd_in[k - GUP], 16)
                act.copy(split_weights(k, gu_hi, wd_hi), raw_weights(k)).then_inc(wgt_hi, 1)

            def spread_values(hv):
                act.wait_ge(v_ps, hv + 1)
                v = bank[7][:].rearrange("p (b d) -> p b d", b=4)
                for px in range(2):
                    src = v.rearrange("p b (j x c d) -> p (b j) x c d", j=4, x=2, c=2)[:, :, px]
                    dst = vblk[:, hv * 32:hv * 32 + 32, px, 0:DK].rearrange("p (n c) d -> p n c d", c=2)
                    act.activation(dst, src, ACT.Copy, scale=halfmask[:, px:px + 1]).then_inc(vblk_ok, 1)

            def probT_copy(b):
                act.wait_ge(pT_ps, b + 1)
                if b >= 2:
                    act.wait_ge(pv_ps, b - 1)
                act.copy(probT[:, b % 2], bank[6][:]).then_inc(pT_ok, 1)

            def ctx_copy(m, banks):
                act.wait_ge(cT_ps, m + 1)
                if m >= 2:
                    act.wait_ge(o_ps, m - 1)
                act.copy(cnT[:, m % 2], turn(banks, m)[:, 0:D]).then_inc(cT_ok, 1)

            def round_h(n):
                w = CH[n % 3][1]
                act.wait_ge(h_ok, n + 1)
                if n >= HS:
                    act.wait_ge(y_ps, (n - HS) // 3 + 1)
                act.copy(h_hi[0:w, n % HS], hg[0:w, n % 2]).then_inc(hi_ok, 1)

            def gate_tanh(n):
                w = CH[n % 3][1]
                act.wait_ge(g_ps, n + 1)
                if n >= 2:
                    act.wait_ge(a_ok, n - 1)
                act.activation(tg[0:w, n % 2], bank[n % 2][0:w, :], ACT.Tanh, scale=0.5).then_inc(t_ok, 1)

            def weight_copy(e):
                act.wait_ge(wB_ps, e + 1)
                act.copy(wB[:, e % 2], bank[4][:]).then_inc(wB_ok, 1)

            def attend(n, at):
                if n == 1:
                    act.wait_ge(xnT_ps, 1)
                    act.copy(xnT[:], bank[5][:]).then_inc(xnT_ok, 1)
                if n == 2:
                    act.wait_ge(q_ps, 1)
                    act.activation(qsq[:], bank[6][:], ACT.Square, bias=bqk[:, 0:1]).then_inc(qsq_ok, 1)
                    act.activation(q[:], bank[6][:], ACT.Identity, bias=bqk[:, 0:1]).then_inc(q_ok, 1)
                for j in at["keys"].get(n, ()):
                    act.wait_ge(k_ps, 1)
                    act.wait_ge(c_zero, 1)
                    r = slice(32 * j, 32 * j + 32)
                    act.activation(kquad[r, j], bank[7][r, :], ACT.Identity,
                                   bias=bqk[r, 1:2]).then_inc(k_ok, 1)
                if n in at["spread"]:
                    spread_values(at["spread"][n])

            def exponentials(b):
                act.wait_ge(sub_ok, b + 1)
                act.activation(prob[:, b % 2], prob[:, b % 2], ACT.Exp, scale=SCALE).then_inc(exp_ok, 1)

            def iteration(experts, attention, finishing=False):
                at = BESIDE if experts else ALONE
                for n in range(NS):
                    if experts and n == 7:
                        if finishing:
                            act.wait_ge(fin_ok, 1)
                        act.copy(x2keep, x2[:]).then_inc(keep_ok, 1)
                    if attention and n in at["probs"]:
                        probT_copy(at["probs"][n])
                    if attention and n in at["project"]:
                        ctx_copy(at["project"][n], at["context_banks"])
                    if experts:
                        if n in DOWN_AT:
                            weight_copy(DOWN_AT[n])
                        gate_tanh(n)
                        if n == NS - 1:
                            weight_copy(E - 1)
                    if attention and n in at["transposes"]:
                        exponentials(at["transposes"][n])
                    if experts:
                        if n == 0:
                            act.wait_ge(lgT_ps, 1)
                            act.copy(lgT, bank[6][0:8, :]).then_inc(lgT_ok, 1)
                        if n >= 1:
                            round_h(n - 1)
                        if n == WT_AT:
                            act.wait_ge(wT_ps, 1)
                            act.copy(WT[:], bank[4][0:16, :]).then_inc(wT_ok, 1)
                        if n == PICK_AT + 1:
                            act.wait_ge(dif_ok, 1)
                            act.activation(ldif[:], ldif[:], ACT.Exp).then_inc(exps_ok, 1)
                    if attention:
                        attend(n, at)
                    if not experts and n in SPLIT_AT:
                        weights_hi(SPLIT_AT[n])
                if experts:
                    round_h(NS - 1)
                if attention:
                    act.wait_ge(xn2T_ps, 1)
                    if experts:
                        act.wait_ge(u_ps, NS)
                    act.copy(xhi[:], bank[6][:]).then_inc(xhi_ok, 1)

            iteration(False, True)
            meet(act)
            iteration(True, True)
            meet(act)
            with act.Fori(2, NG):
                iteration(True, True, True)
                meet(act)
            iteration(True, False, True)

        @block.vector
        def _(dve):
            dve.memset(kquad[:], 0.0).then_inc(c_zero, 1)
            dve.memset(vblk[:], 0.0).then_inc(c_zero, 1)
            dve.memset(W[:], 0.5).then_inc(c_zero, 1)
            dve.memset(halfmask[:], 0.0).then_inc(c_zero, 1)
            dve.memset(bv_parts[:], 0.0).then_inc(c_zero, 1)
            dve.memset(ones[:], 1.0).then_inc(c_zero, 1)
            dve.wait_ge(c_zero, 6)
            dve.memset(halfmask[0:64, 0:1], 1.0).then_inc(c_zero, 1)
            dve.memset(halfmask[64:128, 1:2], 1.0).then_inc(c_zero, 1)
            dve.memset(vblk[0:64, :, 0, DK:VW], 1.0).then_inc(c_zero, 1)
            dve.memset(vblk[64:128, :, 1, DK:VW], 1.0).then_inc(c_zero, 1)
            def masks():
                dve.wait_ge(c_ident, 1)
                dve.tensor_reduce(picked[:], ident[:].rearrange("p (b j r) -> p b r j", b=GB, j=4), AX.X,
                                  ALU.add).then_inc(c_zero, 1)
                dve.tensor_reduce(quadmask[:], ident[:].rearrange("p (b j r) -> p j b r", b=GB, j=4), AX.XY,
                                  ALU.add).then_inc(c_zero, 1)
                dve.wait_ge(c_zero, 12)
                dve.tensor_copy(quadpick[:], picked[:].unsqueeze(3).broadcast_to([P, GB, 4, L])).then_inc(c_zero, 1)
                dve.wait_ge(c_masks, 1)
                dve.tensor_reduce(rowmask[:], headsum[:, 0, 0:H].rearrange("p (j r) -> p r j", r=4), AX.X,
                                  ALU.add).then_inc(rowmask_ok, 1)

            def router_pick():
                dve.wait_ge(c_pick, 1)
                dve.tensor_copy(pick16[:], pick16f).then_inc(pick_ok, 1)

            def first_stats():
                for m in range(NT):
                    i = dve.bn_stats(stats[:, m], xg[:, m])
                i.then_inc(bn_ok, 1)
                dve.wait_ge(bn_ok, 1)
                for m in range(NT):
                    i = dve.bn_aggr(mv[:, m], stats[:, m])
                i.then_inc(mv_ok, 1)
                dve.wait_ge(mv_ok, 1)
                dve.tensor_scalar(ve[:], mv[:, :, 1], EPS, None, ALU.add).then_inc(var_ok, 1)

            def first_norm():
                dve.wait_ge(rstd_ok, 1)
                for m in range(NT):
                    i = dve.tensor_scalar(xn[:, m], xg[:, m], mv[:, m, 0:1], rstd[:, m:m + 1],
                                          ALU.subtract, ALU.mult)
                i.then_inc(xn_ok, 1)

            def once():
                dve.wait_ge(small_in, 16 * 7)
                dve.wait_ge(tgate_ok, 1)
                dve.tensor_scalar(tbo[:], bo_b[:], tgate[:, 0:1], None, ALU.mult).then_inc(tbo_ok, 1)
                dve.wait_ge(c_gp, 3)
                dve.tensor_copy(wr_hi[:], wr_sb[:]).then_inc(wr_ok, 1)
                dve.wait_ge(wr_ok, 1)
                dve.tensor_tensor(wr_lo[:], wr_sb[:], wr_hi[:].bitcast(F32), ALU.subtract).then_inc(wr_ok, 1)

            def split_bias():
                rest = bv_b
                for k in range(3):
                    row = slice(32 * k, 32 * k + 1)
                    dve.tensor_copy(bv_part[:, k], rest[:]).then_inc(bv_split, 1)
                    dve.wait_ge(bv_split, 2 * k + 1)
                    dve.tensor_copy(bv_parts[row], bv_part[row, k]).then_inc(bv_ok, 1)
                    if k < 2:
                        dve.tensor_tensor(bv_rest[:], rest[:], bv_part[:, k], ALU.subtract).then_inc(bv_split, 1)
                        dve.wait_ge(bv_split, 2 * k + 2)
                    rest = bv_rest

            def choose(half):
                if half == 0:
                    dve.wait_ge(norm_ps, 1)
                for r in (2 * half, 2 * half + 1):
                    src = rest[:, r - 1] if r else bank[5][:, 0:L]
                    dve.max(top8[:, r], src).then_inc(top_ok, 1)
                    dve.wait_ge(top_ok, 2 * r + 1)
                    dve.match_replace(rest[:, r], top8[:, r], src, -1.0).then_inc(top_ok, 1)
                    dve.wait_ge(top_ok, 2 * r + 2)

            def chosen():
                src = rest[:, 3]
                dve.tensor_scalar(bias[:], src, 0.0, -BIG, ALU.is_ge, ALU.mult).then_inc(bias_ok, 1)
                dve.tensor_scalar(seld[:], src.unsqueeze(1).broadcast_to([P, 2, L]), 0.0, None,
                                  ALU.is_lt).then_inc(seld_ok, 1)
                dve.wait_ge(bias_ok, 1)
                dve.tensor_tensor(keybias[:], bias[:].unsqueeze(1).broadcast_to([P, 4, L]),
                                  quadmask[:].unsqueeze(2).broadcast_to([P, 4, L]), ALU.mult).then_inc(mask_ok, 1)

            def query_mask():
                dve.wait_ge(selT_ps, 1)
                sT = bank[6][:, 0:P].rearrange("p (m x h) -> p m x h", m=NT, x=2)
                dve.tensor_copy(selP[0:64], sT[0:64, :, 0]).then_inc(selP_ok, 1)
                dve.tensor_copy(selP[64:128], sT[64:128, :, 1]).then_inc(selP_ok, 1)

            def normalise(m, banks):
                dve.wait_ge(pv_ps, 2 * m + 2)
                c = turn(banks, m)[:, 0:H * VW].rearrange("p (n v) -> p n v", v=VW)
                dve.reciprocal(rec[:, m % 2], c[:, :, DK]).then_inc(rec_ok, 1)
                dve.wait_ge(rec_ok, m + 1)
                dve.wait_ge(selP_ok, 2)
                dve.tensor_tensor(recs[:, m % 2].rearrange("p (j c x) -> p j c x", j=4, c=2),
                                  rec[:, m % 2].rearrange("p (j c x) -> p j c x", j=4, c=2),
                                  selP[:, m].rearrange("p (j x c) -> p j c x", j=4, x=2),
                                  ALU.mult).then_inc(recs_ok, 1)
                dve.wait_ge(recs_ok, m + 1)
                if m >= 2:
                    dve.wait_ge(cT_ps, m - 1)
                dve.tensor_tensor(cn[:, m % 2].rearrange("p (n d) -> p n d", d=DK), c[:, :, 0:DK],
                                  recs[:, m % 2].unsqueeze(2).broadcast_to([P, H, DK]),
                                  ALU.mult).then_inc(cn_ok, 1)

            def residual(m, keeping, banks):
                dve.wait_ge(o_ps, m + 1)
                dve.wait_ge(xpb_ok, 1)
                if keeping and m == 0:
                    dve.wait_ge(keep_ok, 1)
                dve.scalar_tensor_tensor(x2[:, m], turn(banks, m)[:, 0:D], tgate[:, 0:1], xpb[:, m],
                                         ALU.mult, ALU.add).then_inc(x2_ok, 1)
                dve.wait_ge(x2_ok, m + 1)
                dve.bn_stats(stats2[:, m], x2[:, m]).then_inc(bn2_ok, 1)
                dve.wait_ge(bn2_ok, m + 1)
                dve.bn_aggr(mv2[:, m], stats2[:, m]).then_inc(mv2_ok, 1)

            def softmax_shift(b, banks):
                sc = turn(banks, b)[:].rearrange("p (n k) -> p n k", n=8)
                dve.wait_ge(s_ps, b + 1)
                dve.tensor_reduce(mx[:, b % 2], sc, AX.X, ALU.max).then_inc(mx_ok, 1)
                dve.wait_ge(mx_ok, b + 1)
                if b >= 2:
                    dve.wait_ge(pT_ps, b - 1)
                dve.tensor_tensor(prob[:, b % 2], sc, mx[:, b % 2].unsqueeze(2).broadcast_to([P, 8, L]),
                                  ALU.subtract).then_inc(sub_ok, 1)

            def second_var(k):
                dve.wait_ge(mv2_ok, LATE[k].stop)
                dve.tensor_scalar(ve2[:, LATE[k]], mv2[:, LATE[k], 1], EPS, None, ALU.add).then_inc(var2_ok, 1)

            def second_norm(k):
                dve.wait_ge(rstd2_ok, k + 1)
                for m in range(LATE[k].start, LATE[k].stop):
                    i = dve.tensor_scalar(xn2[:, m], x2[:, m], mv2[:, m, 0:1], rstd2[:, m:m + 1],
                                          ALU.subtract, ALU.mult)
                i.then_inc(xn2_ok, 1)

            def take_logits():
                dve.wait_ge(lg_ps, 1)
                dve.tensor_tensor(lg[:], bank[6][:, 0:NT * 8].rearrange("p (m e) -> p m e", e=8),
                                  rb_b[:].unsqueeze(1).broadcast_to([P, NT, 8]), ALU.add).then_inc(lg_ok, 1)


            def pick_experts():
                dve.wait_ge(lg_ok, 1)
                for m in range(NT):
                    i = dve.max(ltop[:, m], lg[:, m])
                i.then_inc(rt_ok, 1)
                dve.wait_ge(rt_ok, 1)
                dve.tensor_copy(ltwo[:, :, 0:2], ltop[:, :, 0:2]).then_inc(rt_ok, 1)
                dve.tensor_tensor(ldif[:], lg[:], ltop[:, :, 0:1].broadcast_to([P, NT, 8]),
                                  ALU.subtract).then_inc(dif_ok, 1)
                dve.wait_ge(rt_ok, 2)
                for m in range(NT):
                    i = dve.match_replace(lmark[:, m], ltwo[:, m], lg[:, m], 3 * HUGE)
                i.then_inc(rt_ok, 1)

            def expert_weights():
                dve.wait_ge(rt_ok, 3)
                dve.wait_ge(exps_ok, 1)
                dve.scalar_tensor_tensor(lpick[:], lmark[:], HUGE, ldif[:], ALU.is_ge, ALU.mult).then_inc(w_ok, 1)
                dve.wait_ge(w_ok, 1)
                dve.tensor_reduce(lsum[:], lpick[:], AX.X, ALU.add).then_inc(w_ok, 1)
                dve.wait_ge(w_ok, 2)
                dve.reciprocal(lrec[:], lsum[:]).then_inc(w_ok, 1)
                dve.wait_ge(w_ok, 3)
                dve.scalar_tensor_tensor(W[:, :, 1:8], lpick[:, :, 0:7], 0.5,
                                         lrec[:].unsqueeze(2).broadcast_to([P, NT, 7]),
                                         ALU.mult, ALU.mult).then_inc(w_ok, 1)
                dve.wait_ge(w_ok, 4)
                dve.tensor_copy(whi[:], W[:]).then_inc(w_ok, 1)
                dve.wait_ge(w_ok, 5)
                dve.tensor_copy(W16[:, :, 0:8], whi[:].bitcast(F32))
                dve.tensor_tensor(W16[:, :, 8:16], W[:], whi[:].bitcast(F32), ALU.subtract).then_inc(var_w, 1)

            def weigh(e):
                dve.wait_ge(y_ps, e + 1)
                dve.wait_ge(wB_ok, e + 1)
                if e >= 1:
                    dve.wait_ge(acc_ok, e)
                dve.tensor_tensor(yw, bank[4][:], wB[:, e % 2], ALU.mult).then_inc(yw_ok, 1)

            def hidden(n):
                w = CH[n % 3][1]
                dve.wait_ge(t_ok, n + 1)
                dve.scalar_tensor_tensor(ag[0:w, n % 2], tg[0:w, n % 2], 1.0, bank[n % 2][0:w, :],
                                         ALU.add, ALU.mult).then_inc(a_ok, 1)
                dve.wait_ge(a_ok, n + 1)
                dve.wait_ge(u_ps, n + 1)
                if n >= 2:
                    dve.wait_ge(lo_ok, n - 1)
                dve.tensor_tensor(hg[0:w, n % 2], ag[0:w, n % 2], bank[2 + n % 2][0:w, :],
                                  ALU.mult).then_inc(h_ok, 1)

            def finish(k):
                dve.wait_ge(fT_ps, k)
                if k > 1:
                    dve.wait_ge(keep_ok, 1)
                    dve.wait_ge(out_done, 16)
                dve.scalar_tensor_tensor(fin, bank[4][:].rearrange("p (m d) -> p m d", m=NT), tgate[:, 1:2],
                                         x2keep, ALU.mult, ALU.add).then_inc(fin_ok, 1)

            def attend(n, at):
                if n == CHOOSE_AT:
                    choose(0)
                if n == CHOOSE_AT + 1:
                    choose(1)
                if n == CHOOSE_AT + 3:
                    chosen()
                if n == CHOOSE_AT + 4:
                    query_mask()
                if n in at["project"]:
                    residual(at["project"][n], at is BESIDE, at["context_banks"])
                if n in at["scores"]:
                    softmax_shift(at["scores"][n], at["score_banks"])
                if n in SECOND_VAR_AT:
                    second_var(SECOND_VAR_AT[n])
                if n == min(SECOND_VAR_AT) + 1:
                    second_norm(0)

            def iteration(experts, attention, finishing):
                at = BESIDE if experts else ALONE
                for n in range(NS):
                    if attention and n == 0:
                        first_stats()
                    if attention and n in at["normalise"]:
                        normalise(at["normalise"][n], at["context_banks"])
                    if experts:
                        if n in WEIGH_AT and n < NS - 1:
                            weigh(WEIGH_AT[n])
                        if n == WT_AT - 1:
                            expert_weights()
                        hidden(n)
                        if n + 1 in WEIGH_AT and n + 1 == NS - 1:
                            weigh(WEIGH_AT[n + 1])
                        if attention and n == NS - 1:
                            second_norm(1)
                        if n == 1:
                            take_logits()
                        if n == 2 and finishing:
                            finish(1)
                        if n == PICK_AT:
                            pick_experts()
                    elif n == NS - 1:
                        second_norm(1)
                    if attention and n == 0:
                        first_norm()
                    if attention:
                        if not experts and n == 1:
                            once()
                            masks()
                            split_bias()
                            router_pick()
                        attend(n, at)
                if experts:
                    dve.wait_ge(hi_ok, NS)
                    w = CH[-1][1]
                    dve.tensor_tensor(h_lo[0:w, (NS - 1) % HS], hg[0:w, (NS - 1) % 2],
                                      h_hi[0:w, (NS - 1) % HS].bitcast(F32), ALU.subtract).then_inc(lo_last, 1)
                if attention:
                    dve.wait_ge(xhi_ok, 1)
                    dve.tensor_tensor(xlo[:], bank[6][:], xhi[:].bitcast(F32), ALU.subtract)
                if experts:
                    weigh(E - 1)

            dve.wait_ge(x_in, 16)
            iteration(False, True, False)
            meet(dve)
            iteration(True, True, False)
            meet(dve)
            with dve.Fori(2, NG):
                iteration(True, True, True)
                meet(dve)
            iteration(True, False, True)
            dve.wait_ge(acc_ok, E - 1)
            dve.wait_ge(yw_ok, E)
            dve.tensor_tensor(acc, acc, yw, ALU.add).then_inc(acc_ok, 1)
            finish(2)

        @block.tensor
        def _(pe):
            def values(hv):
                if hv:
                    pe.wait_ge(vblk_ok, 2)
                else:
                    pe.wait_ge(k_ok, 4)
                pe.matmul(bank[7][:], ones[:], bv_parts[:].unsqueeze(1).broadcast_to([P, 4, D]),
                          start=True, stop=False)
                for b in range(4):
                    i = pe.matmul(bank[7][:, b * D:(b + 1) * D],
                                  ctx[:, hv * 4 + b].rearrange("p a l -> p (a l)"), wv_sb[:],
                                  start=False, stop=b == 3)
                i.then_inc(v_ps, 1)

            def scores(b, banks):
                pe.wait_ge(qexp_ok, b + 1)
                if b == 0:
                    pe.wait_ge(mask_ok, 1)
                if b >= len(banks):
                    pe.wait_ge(sub_ok, b - len(banks) + 1)
                for pp in range(2):
                    dst = turn(banks, b)[:].rearrange("p (j x k) -> p j x k", j=4, x=2)[:, :, pp]
                    pair = slice(2 * pp, 2 * pp + 2)
                    pe.matmul(dst, qexp[:, b, pair], kquad[:, :, b * L:(b + 1) * L],
                              start=True, stop=False)
                    i = pe.matmul(dst, quadpick[:, b, pair].rearrange("p a l -> p (a l)"),
                                  keybias[:], start=False, stop=True)
                i.then_inc(s_ps, 1)

            def prob_transposes(b):
                pe.wait_ge(exp_ok, b + 1)
                if b == 0:
                    pe.wait_ge(selP_ok, 2)
                else:
                    pe.wait_ge(pT_ok, b)
                for j in range(4):
                    i = pe.transpose(bank[6][:, j * P:(j + 1) * P],
                                     prob[:, b % 2, 2 * j:2 * j + 2].rearrange("p a k -> p (a k)"), ident[:])
                i.then_inc(pT_ps, 1)

            def context(b, banks):
                pe.wait_ge(pT_ok, b + 1)
                pe.wait_ge(vblk_ok, 2 * (b // 4) + 2)
                if b == 0:
                    pe.wait_ge(vblk_ok, 4)
                elif b % 2 == 0 and b // 2 >= len(banks):
                    pe.wait_ge(x2_ok, b // 2 - len(banks) + 1)
                r = slice(64 * (b % 2), 64 * (b % 2) + 64)
                for n in range(8):
                    i = pe.matmul(turn(banks, b // 2)[r, n * 2 * VW:(n + 1) * 2 * VW], probT[:, b % 2, n * 64:(n + 1) * 64],
                                  vblk[:, b * 8 + n].rearrange("p x v -> p (x v)"), start=True, stop=True)
                i.then_inc(pv_ps, 1)

            def ctx_transpose(m, banks):
                pe.wait_ge(cn_ok, m + 1)
                pe.transpose(turn(banks, m)[:, 0:D], cn[:, m % 2], ident[:]).then_inc(cT_ps, 1)

            def project(m, banks):
                pe.wait_ge(cT_ok, m + 1)
                pe.matmul(turn(banks, m)[:, 0:D], cnT[:, m % 2], wo_sb[:], start=True, stop=True).then_inc(o_ps, 1)

            def second_transposes():
                pe.wait_ge(xn2_ok, 2)
                pe.wait_ge(pT_ok, GB)
                for m in range(NT):
                    i = pe.transpose(bank[6][:, m * P:(m + 1) * P], xn2[:, m], ident[:])
                i.then_inc(xn2T_ps, 1)

            def logits():
                for k, (w, xx) in enumerate(((wr_hi, xhi), (wr_hi, xlo), (wr_lo, xhi))):
                    i = pe.matmul(bank[6][0:8, :], w[:], xx[:], start=k == 0, stop=k == 2)
                i.then_inc(lgT_ps, 1)

            def logit_transposes():
                pe.wait_ge(lgT_ok, 1)
                for m in range(NT):
                    i = pe.transpose(bank[6][:, m * 8:(m + 1) * 8], lgT[:, m * P:(m + 1) * P], ident[0:8, 0:8])
                i.then_inc(lg_ps, 1)

            def weight_transposes():
                pe.wait_ge(var_w, 1)
                for m in range(NT):
                    i = pe.transpose(bank[4][0:16, m * P:(m + 1) * P], W16[:, m], ident[:])
                i.then_inc(wT_ps, 1)

            def spread_weight(e):
                if e == 0:
                    pe.wait_ge(wT_ok, 1)
                else:
                    pe.wait_ge(yw_ok, e)
                pe.matmul(bank[4][:], pick16[:, e], WT[:], start=True, stop=True).then_inc(wB_ps, 1)

            def gate_up(n, between=None):
                e, c = n // 3, n % 3
                c0, w = CH[c]
                if n >= 2:
                    pe.wait_ge(h_ok, n - 1)
                for part, (bk_, sem_) in enumerate(((n % 2, g_ps), (2 + n % 2, u_ps))):
                    o = (e * 2 + part) * I + c0
                    for k, (wt, xx) in enumerate(((gu_hi, xhi), (gu_hi, xlo), (gu_lo, xhi))):
                        i = pe.matmul(bank[bk_][0:w, :], wt[:, o:o + w], xx[:], start=k == 0, stop=k == 2)
                    i.then_inc(sem_, 1)
                    if between is not None and part == 0:
                        between()

            def down(e, between=None):
                pe.wait_ge(wB_ok, e + 1)
                for c in range(3):
                    if between is not None and c == 1:
                        between()
                    if 3 * e + c < NS - 1:
                        pe.wait_ge(lo_ok, 3 * e + c + 1)
                    else:
                        pe.wait_ge(lo_last, 1)
                    w = CH[c][1]
                    sl = (3 * e + c) % HS
                    for k, (wt, hh) in enumerate(((wd_hi, h_hi), (wd_hi, h_lo), (wd_lo, h_hi))):
                        i = pe.matmul(bank[4][:], wt[0:w, c, e * D:(e + 1) * D], hh[0:w, sl],
                                      start=c == 0 and k == 0, stop=c == 2 and k == 2)
                i.then_inc(y_ps, 1)

            def sum_transposes(k):
                if k > 1:
                    pe.wait_ge(acc_ok, E)
                for m in range(NT):
                    i = pe.transpose(bank[4][:, m * P:(m + 1) * P], acc[:, m * P:(m + 1) * P], ident[:])
                i.then_inc(fT_ps, 1)

            def attend(n, at):
                if n == 1:
                    pe.wait_ge(xn_ok, 1)
                    for m in range(NT):
                        i = pe.transpose(bank[5][:, m * P:(m + 1) * P], xn[:, m], ident[:])
                    i.then_inc(xnT_ps, 1)
                    pe.matmul(bank[7][:], wk_sb[:], ctx[:, :, 0], start=True, stop=True).then_inc(k_ps, 1)
                if n == 2:
                    pe.wait_ge(xnT_ok, 1)
                    pe.matmul(bank[6][:], wq_sb[:], xnT[:], start=True, stop=True).then_inc(q_ps, 1)
                if n == 3:
                    pe.wait_ge(qsq_ok, 1)
                    for b in range(GB):
                        i = pe.matmul(bank[5][:, 0:L], headsum[:, b], qsq[:, b * L:(b + 1) * L],
                                      start=b == 0, stop=b == GB - 1)
                    i.then_inc(norm_ps, 1)
                if n in at["values"]:
                    values(at["values"][n])
                if n == CHOOSE_AT + 4:
                    pe.wait_ge(seld_ok, 1)
                    pe.transpose(bank[6][:, 0:P], seld[:].rearrange("p a l -> p (a l)"),
                                 ident[:]).then_inc(selT_ps, 1)
                if n in at["scores"]:
                    scores(at["scores"][n], at["score_banks"])
                if n in at["normalise"]:
                    ctx_transpose(at["normalise"][n], at["context_banks"])
                if n in at["context"]:
                    for b in range(2 * at["context"][n], 2 * at["context"][n] + 2):
                        context(b, at["context_banks"])
                if n in at["transposes"]:
                    prob_transposes(at["transposes"][n])

            def iteration(experts, attention, finishing):
                at = BESIDE if experts else ALONE
                for n in range(NS):
                    if experts:
                        gate_up(n, (lambda: spread_weight(E - 1)) if n == NS - 1 else None)
                        if n == 0:
                            logits()
                        if n == 1:
                            logit_transposes()
                            if finishing:
                                pe.wait_ge(last_ok, 1)
                                sum_transposes(1)
                        if n == WT_AT:
                            if finishing:
                                pe.wait_ge(fin_ok, 1)
                            weight_transposes()
                    if attention and n in at["project"]:
                        project(at["project"][n], at["context_banks"])
                    if experts and n in DOWN_AT:
                        down(DOWN_AT[n])
                    if attention:
                        if experts and n == 2:
                            pe.wait_ge(lg_ok, 1)
                        if not experts:
                            if n == 3:
                                pe.wait_ge(c_masks, 1)
                            if at["values"].get(n) == 0:
                                pe.wait_ge(bv_ok, 3)
                            if n == 8:
                                pe.wait_ge(c_zero, 13)
                        attend(n, at)
                    if experts and n in SPREAD_AT:
                        spread_weight(SPREAD_AT[n])
                if experts:
                    down(E - 1, second_transposes if attention else None)
                elif attention:
                    second_transposes()

            pe.wait_ge(c_ident, 1)
            pe.wait_ge(wqkv_in, 64)
            pe.wait_ge(ctx_in, 32)
            iteration(False, True, False)
            meet(pe)
            pe.wait_ge(wr_ok, 2)
            pe.wait_ge(pick_ok, 1)
            pe.wait_ge(wgt_lo, GUP + NC_)
            iteration(True, True, False)
            meet(pe)
            with pe.Fori(2, NG):
                iteration(True, True, True)
                meet(pe)
            iteration(True, False, True)
            pe.wait_ge(yw_ok, E)
            sum_transposes(2)


def kernel(**inputs):
    import numpy as np
    import concourse.bacc as bacc
    from concourse import mybir as _mybir
    from concourse.bass_utils import run_bass_kernel_spmd as run

    a = {k: np.asarray(v) for k, v in inputs.items()}
    heads = np.arange(D).reshape(4, 2, 2, DK).transpose(0, 2, 1, 3).reshape(-1)
    gate = np.concatenate([a["L0_ffn_sg"][None], a["L0_ffn_rg"]])
    up = np.concatenate([a["L0_ffn_su"][None], a["L0_ffn_ru"]])
    down = np.concatenate([a["L0_ffn_sd"][None], a["L0_ffn_rd"]])
    arrays = {
        "x": a["x"].reshape(B * L, D),
        "ctxT": a["ctx_1024"].reshape(B * L, D).T,
        "gates": np.concatenate([a["g_xattn"], a["g_ffn"]]),
        "wq": a["L0_xattn_Wq"], "bq": a["L0_xattn_bq"], "wk": a["L0_xattn_Wk"], "bk": a["L0_xattn_bk"],
        "wv": a["L0_xattn_Wv"], "bv": a["L0_xattn_bv"], "wo": a["L0_xattn_Wo"][heads], "bo": a["L0_xattn_bo"],
        "wgu": np.stack([gate, up], 1).transpose(3, 0, 1, 2).reshape(D, -1),
        "wd": down.transpose(0, 2, 1),
        "wrT": a["L0_ffn_wr"].T, "rb": a["L0_ffn_rb"],
    }
    arrays = {k: np.ascontiguousarray(v) for k, v in arrays.items()}
    nc = bacc.Bacc("TRN2", target_bir_lowering=False, num_devices=1)
    args = [nc.dram_tensor(f"in_{k}", v.shape, _mybir.dt.from_np(v.dtype), kind="ExternalInput").ap()
            for k, v in arrays.items()]
    y = nc.dram_tensor("out_y", (B * L, D), _mybir.dt.float32, kind="ExternalOutput").ap()
    gated_block(nc, *args, y)
    r = run(nc, [{f"in_{k}": v for k, v in arrays.items()}], core_ids=[0])
    return r.results[0]["out_y"].reshape(B, L, D)
```
